# Optimizing a Trainium2 kernel written in Bass

```python
import numpy as np
import jax
import jax.numpy as jnp

def _softmax(x, axis=-1):
    return jax.nn.softmax(x, axis=axis)

def _gelu(x):
    return jax.nn.gelu(x, approximate=True)

def _silu(x):
    return jax.nn.silu(x)

def _sigmoid(x):
    return jax.nn.sigmoid(x)

def _layernorm(x, axis=-1, eps=1e-05):
    m = jnp.mean(x, axis=axis, keepdims=True)
    v = jnp.var(x, axis=axis, keepdims=True)
    return (x - m) / jnp.sqrt(v + eps)

def _scatter_add(tgt, idx, src, axis=0):
    return tgt.at[idx].add(src)

def _segment_sum(src, seg, n):
    return jax.ops.segment_sum(src, seg, n)
kernel_name = 'mk_cond_resid_d2_seqx_r4_b4075b'

def setup_inputs(seed: int=0):
    np.random.seed(seed)
    _w = jnp.asarray

    def _rec_inputs():
        import jax
        import jax.numpy as jnp
        _rk = jax.random.key(seed)
        x = -0.000125 + 0.9999 * jax.random.normal(jax.random.fold_in(_rk, 1), (64, 64, 256), jnp.float32)
        _lenS = 64 - jax.random.randint(jax.random.fold_in(_rk, 7), (64,), 0, max(1, 64 // 4) + 1, jnp.int32)
        _lenS2 = 64 - jax.random.randint(jax.random.fold_in(_rk, 8), (64,), 0, max(1, 64 // 4) + 1, jnp.int32)
        cond_1024 = -0.00493535 + 1.00056 * jax.random.normal(jax.random.fold_in(_rk, 11), (64, 256), jnp.float32)
        return (x, cond_1024)
    x, cond_1024 = _rec_inputs()

    def _L0_cond_setup():
        import jax, jax.numpy as jnp
        from jax import lax
        import numpy as np
        B, T, U = (64, 128, 256)
        key = jax.random.key(seed)
        k1, k2, k3 = jax.random.split(key, 3)
        x = jax.random.normal(k1, (B, T, U), dtype=jnp.float32)
        h0 = jax.random.normal(k2, (B, U), dtype=jnp.float32)
        limit = float(np.sqrt(6.0 / (2 * U + 2 * U)))
        weight = jax.random.uniform(k3, (2 * U, 2 * U), minval=-limit, maxval=limit, dtype=jnp.float32)
        bias = jnp.zeros((2 * U,), dtype=jnp.float32)
        return {'x': x, 'h0': h0, 'weight': weight, 'bias': bias}
    _L0_cond_all = _L0_cond_setup()
    _L0_cond_in = {k: v for k, v in _L0_cond_all.items() if k in ('weight', 'bias')}
    del _L0_cond_all

    def _L1_cond_setup():
        import jax, jax.numpy as jnp
        import numpy as np
        NUM_EXPERTS = 4
        TOP_K = 2
        key = jax.random.key(seed)
        ks = jax.random.split(key, 16)
        B, L, D, E, H = (8, 192, 256, NUM_EXPERTS, 1024)
        s = 0.02
        return {'context_c': jax.random.normal(ks[0], (B, L, D), jnp.float32), 'time_cond': jax.random.normal(ks[1], (B, D), jnp.float32), 'gate_w': jax.random.normal(ks[2], (3 * D, E), jnp.float32) * s, 'gate_b': jnp.zeros((E,), jnp.float32), 'time_w': jax.random.normal(ks[3], (D, 2 * E), jnp.float32) * s, 'time_b': jnp.zeros((2 * E,), jnp.float32), 'ew1': jax.random.normal(ks[4], (E, D, H), jnp.float32) * s, 'eb1': jnp.zeros((E, H), jnp.float32), 'ew2': jax.random.normal(ks[5], (E, H, D), jnp.float32) * s, 'eb2': jnp.zeros((E, D), jnp.float32), 'sw1': jax.random.normal(ks[6], (D, H), jnp.float32) * s, 'sb1': jnp.zeros((H,), jnp.float32), 'sw2': jax.random.normal(ks[7], (H, D), jnp.float32) * s, 'sb2': jnp.zeros((D,), jnp.float32)}
    _L1_cond_all = _L1_cond_setup()
    _L1_cond_in = {k: v for k, v in _L1_cond_all.items() if k in ('gate_w', 'gate_b', 'time_w', 'time_b', 'ew1', 'eb1', 'ew2', 'eb2', 'sw1', 'sb1', 'sw2', 'sb2')}
    del _L1_cond_all
    return {'x': x, 'cond_1024': cond_1024, 'L0_cond_weight': _L0_cond_in['weight'], 'L0_cond_bias': _L0_cond_in['bias'], 'L1_cond_gate_w': _L1_cond_in['gate_w'], 'L1_cond_gate_b': _L1_cond_in['gate_b'], 'L1_cond_time_w': _L1_cond_in['time_w'], 'L1_cond_time_b': _L1_cond_in['time_b'], 'L1_cond_ew1': _L1_cond_in['ew1'], 'L1_cond_eb1': _L1_cond_in['eb1'], 'L1_cond_ew2': _L1_cond_in['ew2'], 'L1_cond_eb2': _L1_cond_in['eb2'], 'L1_cond_sw1': _L1_cond_in['sw1'], 'L1_cond_sb1': _L1_cond_in['sb1'], 'L1_cond_sw2': _L1_cond_in['sw2'], 'L1_cond_sb2': _L1_cond_in['sb2']}

def reference(x, cond_1024, L0_cond_weight, L0_cond_bias, L1_cond_gate_w, L1_cond_gate_b, L1_cond_time_w, L1_cond_time_b, L1_cond_ew1, L1_cond_eb1, L1_cond_ew2, L1_cond_eb2, L1_cond_sw1, L1_cond_sb1, L1_cond_sw2, L1_cond_sb2):
    import jax
    import jax.numpy as jnp

    def _L0_cond_ref(x, h0, weight, bias):
        import jax, jax.numpy as jnp
        from jax import lax
        import numpy as np
        B, T, U = (64, 128, 256)
        'UGRNN cell scanned over time. x:[B,T,U], h0:[B,U] -> outputs [B,T,U].'
        units = h0.shape[-1]

        def step(h, xt):
            cell_inputs = jnp.concatenate([xt, h], axis=-1)
            m = cell_inputs @ weight + bias
            g_act = m[:, :units]
            c_act = m[:, units:]
            c = jnp.tanh(c_act)
            g = jax.nn.sigmoid(g_act + 1.0)
            h_new = g * h + (1.0 - g) * c
            return (h_new, h_new)
        xs = jnp.swapaxes(x, 0, 1)
        _, ys = lax.scan(step, h0, xs)
        return jnp.swapaxes(ys, 0, 1)

    def _L1_cond_ref(context_c, time_cond, gate_w, gate_b, time_w, time_b, ew1, eb1, ew2, eb2, sw1, sb1, sw2, sb2):
        import jax, jax.numpy as jnp
        import numpy as np
        NUM_EXPERTS = 4
        TOP_K = 2
        B, L, D = context_c.shape
        E, K = (NUM_EXPERTS, TOP_K)
        L_head = L_wrist = L // 3
        head = context_c[:, :L_head]
        wrist = context_c[:, L_head:L_head + L_wrist]
        proprio = context_c[:, L_head + L_wrist:]
        full_agg = context_c.mean(axis=1)
        hp_agg = jnp.concatenate([head, proprio], axis=1).mean(axis=1)
        wp_agg = jnp.concatenate([wrist, proprio], axis=1).mean(axis=1)
        gate_in = jnp.concatenate([full_agg, hp_agg, wp_agg], axis=-1)
        gate_logits = gate_in @ gate_w + gate_b
        mod = jax.nn.silu(time_cond) @ time_w + time_b
        scale, shift = jnp.split(mod, 2, axis=-1)
        gate_logits = gate_logits * (1.0 + scale) + shift
        gate_scores = jax.nn.softmax(gate_logits, axis=-1)
        topk_w, topk_i = jax.lax.top_k(gate_scores, K)
        topk_w = topk_w / (topk_w.sum(axis=-1, keepdims=True) + 1e-08)
        onehot = (topk_i[..., None] == jnp.arange(E)[None, None, :]).astype(context_c.dtype)
        w_be = jnp.sum(topk_w[..., None] * onehot, axis=1)
        mask = np.ones((E, L), dtype=np.float32)
        mask[1, L_head:L_head + L_wrist] = 0.0
        mask[2, :L_head] = 0.0
        mask = jnp.asarray(mask)
        out = jnp.zeros_like(context_c)
        for e in range(E):
            h = jax.nn.gelu(context_c @ ew1[e] + eb1[e], approximate=True)
            y = h @ ew2[e] + eb2[e]
            out = out + w_be[:, e][:, None, None] * mask[e][None, :, None] * y
        shared = jax.nn.gelu(context_c @ sw1 + sb1, approximate=True) @ sw2 + sb2
        return out + shared
    x = x + _L0_cond_ref(x, cond_1024, L0_cond_weight, L0_cond_bias)
    x = x + _L1_cond_ref(x, cond_1024, L1_cond_gate_w, L1_cond_gate_b, L1_cond_time_w, L1_cond_time_b, L1_cond_ew1, L1_cond_eb1, L1_cond_ew2, L1_cond_eb2, L1_cond_sw1, L1_cond_sb1, L1_cond_sw2, L1_cond_sb2)
    return x

_drawn_inputs = setup_inputs


def setup_inputs(seed=0):
    import zlib

    import numpy as np

    out = dict(_drawn_inputs(seed))
    spreads = {'L0_cond_bias': (0.0, 0.1),
     'L1_cond_gate_b': (0.0, 0.1),
     'L1_cond_time_b': (0.0, 0.1),
     'L1_cond_eb1': (0.0, 0.378),
     'L1_cond_eb2': (0.0, 0.1),
     'L1_cond_sb1': (0.0, 0.1),
     'L1_cond_sb2': (0.0, 0.1)}
    factors = {}
    for name, (base, spread) in spreads.items():
        noise = np.random.default_rng([zlib.crc32(name.encode()), seed]).standard_normal(out[name].shape)
        drawn = base * np.exp(spread * noise) if base else spread * noise
        out[name] = jnp.asarray(drawn.astype(out[name].dtype))
    for name, factor in factors.items():
        out[name] = (out[name] * factor).astype(out[name].dtype)
    return out
```

```python
from contextlib import ExitStack

import concourse.bass as bass
from concourse import mybir

F32 = mybir.dt.float32
F32R = mybir.dt.float32r
I32 = mybir.dt.int32
ALU = mybir.AluOpType
ACT = mybir.ActivationFunctionType
AX_X = mybir.AxisListType.X

P = 128
B = 64
T = 64
D = 256
K = D // P
E = 4
HID = 1024
NCH = HID // P
GT = 8
NG = T // GT
GTOK = GT * B
SLOTS = 8
HEAD = T // 3
PROP = T - 2 * HEAD
MAXG = (2 * B + (SLOTS - 1) * E) // SLOTS + 1
NSLOT = MAXG * SLOTS
PIECE = 512
WCOLS = K * HID

RUNS = [[(0, T)], [(0, HEAD), (2 * HEAD, T)], [(HEAD, T)], [(0, T)]]
TOKS = [sum(b - a for a, b in r) for r in RUNS]

C_TRI = 0
C_IOTA = C_TRI + B
C_BIDX = C_IOTA + NSLOT
C_ONES = C_BIDX + 32
C_EIGHTS = C_ONES + P
C_M0 = C_EIGHTS + SLOTS
C_M1 = C_M0 + 1
C_END = C_M1 + 1
S_B1, S_B2, S_GW, S_TW, S_GB, S_TB = 0, 40, 50, 74, 90, 94
S_END = 102


def cond_resid_kernel(nc, x, cond, w0, b0, w_exp, small, consts, out):
    ctx = ExitStack()
    with ctx:
        def sb(name, shape, dt=F32):
            return ctx.enter_context(nc.sbuf_tensor(name, shape, dt))

        def psum(name, shape):
            return ctx.enter_context(nc.psum_tensor(name, shape, F32))

        def sem(name):
            return ctx.enter_context(nc.semaphore(name))

        acc = sb("acc", [P, K, T, B])
        x_hl = sb("x_hl", [P, 2, K, T, B], F32R)
        w_buf = [sb(f"w_buf{i}", [P, 2, 2 * WCOLS], F32R) for i in range(2)]
        shared_buf = sb("shared_buf", [P, 4096], F32R)
        w0_hl = shared_buf[:].rearrange("p (s k n) -> p s k n", s=2, k=2 * K)
        xg = shared_buf[:].rearrange("p (i s k n) -> p i s k n", i=2, s=2, k=K)
        stage = sb("stage", [P, 2, PIECE])
        g_f = sb("g_f", [P, 2, 512])
        g_hi = sb("g_hi", [P, 2, 512], F32R)
        g_lo = sb("g_lo", [P, 2, 512], F32R)
        y_w = sb("y_w", [P, K, 512])
        bias0 = sb("bias0", [P, 512], F32R)
        ones_r = sb("ones_r", [P, 128], F32R)
        uc = sb("uc", [P, 2, K, B])
        d_t = sb("d_t", [P, K, B])
        h_f = sb("h_f", [P, 2, K, B])
        h_hi = sb("h_hi", [P, K, B], F32R)
        h_lo = sb("h_lo", [P, K, B], F32R)
        seg = sb("seg", [P, 3, K, B])
        par = sb("par", [P, S_END])
        con = sb("con", [P, C_END])
        slot_w = sb("slot_w", [P, NSLOT])
        turn = sb("turn", [P, 2])
        gs = sb("gs", [P, 96])
        cmp8 = sb("cmp8", [P, E, SLOTS])
        slot_b = sb("slot_b", [1, NSLOT], I32)
        starts = sb("starts", [P, E + 1], I32)

        y_flat = y_w[:].rearrange("p k n -> p (k n)")
        pick = y_flat[0:B, 0:NSLOT]
        pick_w = y_flat[0:B, NSLOT:2 * NSLOT]
        agg = y_flat[:, 640:640 + 3 * K * B].rearrange("p (i k b) -> p i k b", i=3, k=K)
        z = [psum(f"z{i}", [P, 2, 2 * K, B]) for i in range(2)]
        hp = [psum(f"hp{i}", [P, 512]) for i in range(2)]
        yp = [[psum(f"yp{i}{k}", [P, 512]) for k in range(K)] for i in range(2)]

        mod_f = gs[0:B, 0:8]
        logit = gs[0:B, 8:12]
        nmax = gs[0:B, 12:13]
        ex = gs[0:B, 13:17]
        esum = gs[0:B, 17:18]
        score = gs[0:B, 18:22]
        rank4 = gs[0:B, 22:38].rearrange("p (j e) -> p j e", j=E)
        rank = gs[0:B, 38:42]
        sel = gs[0:B, 42:46]
        wsel = gs[0:B, 46:50]
        den = gs[0:B, 50:51]
        ngr = gs[:, 51:55]
        start_f = gs[:, 55:60]
        gslot = gs[0:B, 60:64]
        cmp_w = slot_w[0:B, :]

        s_cond, s_w0, s_par, s_x0, s_x1, s_out = (sem(n) for n in ("s_cond", "s_w0", "s_par", "s_x0", "s_x1", "s_out"))
        w0_split = sem("w0_split")
        piece_in = [sem(f"piece_in{i}") for i in range(2)]
        piece_hi, piece_done = sem("piece_hi"), sem("piece_done")
        bias_ready, ones_ready = sem("bias_ready"), sem("ones_ready")
        xs_hi, xs_done = sem("xs_hi"), sem("xs_done")
        z_done, tanh_done = sem("z_done"), sem("tanh_done")
        d_done, q_done, hhi_done, h_done, hlo_done = (sem(n) for n in ("d_done", "q_done", "hhi_done", "h_done", "hlo_done"))
        x1_sum, x1_hi, x1_done, seg_done = (sem(n) for n in ("x1_sum", "x1_hi", "x1_done", "seg_done"))
        l1_done, l2_done, y_read = sem("l1_done"), sem("l2_done"), sem("y_read")
        gelu_done, ghi_done, glo_done = sem("gelu_done"), sem("ghi_done"), sem("glo_done")
        silu_t, silu_done, mod_mm = sem("silu_t"), sem("silu_done"), sem("mod_mm")
        agg_done, gate_mm, nmax_done, exp_done = sem("agg_done"), sem("gate_mm"), sem("nmax_done"), sem("exp_done")
        sel_done, pos_mm, pick_done, list_mm, lists_done = (sem(n) for n in ("sel_done", "pos_mm", "pick_done", "list_mm", "lists_done"))
        dve_math = sem("dve_math")
        gather_done, turn_done = sem("gather_done"), sem("turn_done")
        yw_done, add_done, out_ready = sem("yw_done"), sem("add_done"), sem("out_ready")

        block = ctx.enter_context(nc.Block())
        NP = 2 * WCOLS // PIECE
        ORDER = [E] + list(range(E))

        def gather(pool, e, r):
            pool.wait_ge(l1_done, (r + NG - 1) * NCH)
            pool.wait_ge(gather_done, r + 1)
            pool.tensor_tensor(turn[:, 1:2], turn[:, 0:1], turn[:, 0:1], ALU.mult)
            n = TOKS[e]
            for s in range(SLOTS):
                b = pool.value_load(slot_b[0:1, bass.ds(r * SLOTS + s, 1)], min_val=0, max_val=B - 1)
                o = s * n
                for a, z_ in RUNS[e]:
                    src = x_hl[:, :, :, a:z_, bass.ds(b, 1)].rearrange("p s k t b -> p (s k) (t b)")
                    dst = xg[:, bass.ds(r % 2, 1), :, :, o:o + z_ - a].rearrange("p i s k n -> p (i s k) n")
                    last = pool.tensor_copy(dst, src)
                    o += z_ - a
            last.then_inc(gather_done, 1)

        @block.sync
        def _(sp):
            sp.dma_start(h_f[:, 0], cond).then_inc(s_cond, 16)
            sp.dma_start(acc[:, :, 0:GT], x[:, :, 0:GT]).then_inc(s_x0, 16)
            sp.dma_start(g_f[:].rearrange("p i n -> p (i n)"), w0[:, 0:1024]).then_inc(s_w0, 16)
            sp.dma_start(y_w[:].rearrange("p i n -> p (i n)"), w0[:, 1024:2048]).then_inc(s_w0, 16)
            sp.dma_start(par[:], small).then_inc(s_par, 16)
            sp.dma_start(con[:], consts).then_inc(s_par, 16)
            sp.dma_start(stage[:, 0], b0).then_inc(s_par, 16)
            sp.dma_start(acc[:, :, GT:T], x[:, :, GT:T]).then_inc(s_x1, 16)
            for n in range(len(ORDER) * NP):
                if n == 0:
                    sp.wait_ge(bias_ready, 1)
                if n >= 2:
                    sp.wait_ge(piece_done, n - 1)
                e, j = ORDER[n // NP], n % NP
                sp.dma_start(stage[:, n % 2], w_exp[e, :, j * PIECE:(j + 1) * PIECE]).then_inc(piece_in[n % 2], 16)
            sp.wait_ge(out_ready, 1)
            sp.dma_start(out, acc[:]).then_inc(s_out, 16)
            sp.wait_ge(s_out, 16)

        @block.gpsimd
        def _(pool):
            def split_x(s):
                pool.tensor_copy(x_hl[:, 0, :, bass.ds(s, 1), :], acc[:, :, bass.ds(s, 1), :]).then_inc(xs_hi, 1)
                pool.wait_ge(xs_hi, s + 1)
                pool.tensor_tensor(x_hl[:, 1, :, bass.ds(s, 1), :], acc[:, :, bass.ds(s, 1), :],
                                   x_hl[:, 0, :, bass.ds(s, 1), :].bitcast(F32), ALU.subtract).then_inc(xs_done, 1)

            def add_h(s, i):
                a = acc[:, :, bass.ds(s, 1), :].rearrange("p k t b -> p k (t b)")
                hi = x_hl[:, 0, :, bass.ds(s, 1), :].rearrange("p k t b -> p k (t b)")
                lo = x_hl[:, 1, :, bass.ds(s, 1), :].rearrange("p k t b -> p k (t b)")
                sg = seg[:, bass.ds((s * 3 + 2) // 64, 1)].rearrange("p s k b -> p (s k) b")
                pool.wait_ge(h_done, s + 2)
                pool.tensor_tensor(hi, a, h_f[:, 1 - i % 2], ALU.add).then_inc(x1_hi, 1)
                pool.tensor_tensor(a, a, h_f[:, 1 - i % 2], ALU.add).then_inc(x1_sum, 1)
                pool.wait_ge(x1_sum, s + 1)
                pool.tensor_tensor(lo, a, hi.bitcast(F32), ALU.subtract).then_inc(x1_done, 1)
                pool.wait_ge(seg_done, s + 1)
                pool.tensor_tensor(sg, sg, a, ALU.add).then_inc(seg_done, 1)

            def split_piece(n):
                w = w_buf[(n // NP) % 2]
                c = n % NP * PIECE
                pool.wait_ge(piece_in[n % 2], 16 * (n // 2 + 1))
                pool.tensor_copy(w[:, 0, c:c + PIECE], stage[:, n % 2]).then_inc(piece_hi, 1)
                pool.wait_ge(piece_hi, n + 1)
                pool.tensor_tensor(w[:, 1, c:c + PIECE], stage[:, n % 2],
                                   w[:, 0, c:c + PIECE].bitcast(F32), ALU.subtract).then_inc(piece_done, 1)

            pool.memset(turn[:], 0.0).then_inc(gather_done, 1)
            pool.memset(seg[:], 0.0).then_inc(seg_done, 1)
            pool.wait_ge(s_x0, 16)
            for s in range(GT):
                split_x(s)
            pool.wait_ge(s_x1, 16)
            for s in range(GT):
                add_h(s, s)
                split_x(s + GT)
                split_piece(2 * s)
                split_piece(2 * s + 1)
            with pool.Fori(1, NG - 1) as g:
                for i in range(GT):
                    add_h(g * GT + i, i)
                    split_x(g * GT + GT + i)
            for i in range(GT):
                add_h((NG - 1) * GT + i, i)

            pool.wait_ge(lists_done, 3)
            sv = [pool.value_load(starts[0:1, e:e + 1], min_val=0, max_val=MAXG) for e in range(E + 1)]
            for e in range(E):
                if e:
                    pool.wait_ge(y_read, sv[e - 1] + NG)
                    pool.wait_ge(gather_done, sv[e] + 1)
                    pool.tensor_tensor(turn[:, 1:2], turn[:, 0:1], turn[:, 0:1], ALU.mult).then_inc(turn_done, 1)
                    pool.wait_ge(turn_done, e)
                    for j in range(NP):
                        split_piece((e + 1) * NP + j)
                with pool.Fori(sv[e], sv[e + 1]) as r:
                    g = r + NG
                    gather(pool, e, r)

        def gelu_chunk(act, g, j, e, n):
            c = g * NCH + j
            act.wait_ge(l1_done, c + 1)
            if not (isinstance(g, int) and g == 0 and j < 2):
                act.wait_ge(glo_done, c - 1)
            act.activation(g_f[:, j % 2, 0:n], hp[j % 2][:, 0:n], ACT.Gelu_apprx_tanh,
                           bias=par[:, S_B1 + e * NCH + j:S_B1 + e * NCH + j + 1]).then_inc(gelu_done, 1)
            act.wait_ge(gelu_done, c + 1)
            if not (isinstance(g, int) and g == 0 and j < 2):
                act.wait_ge(l2_done, c - 1)
            act.activation(g_hi[:, j % 2, 0:n], g_f[:, j % 2, 0:n], ACT.Copy).then_inc(ghi_done, 1)

        @block.scalar
        def _(act):
            act.wait_ge(ones_ready, 1)
            act.activation(gs[:, 64:65], ones_r[:, 0:1].bitcast(F32), ACT.Gelu_apprx_tanh)
            act.wait_ge(s_cond, 16)
            act.activation(uc[:, 0], h_f[:, 0], ACT.Tanh, scale=0.5).then_inc(silu_t, 1)

            def tanh(s, i):
                act.wait_ge(z_done, s + 1)
                act.activation(uc[:].rearrange("p u k b -> p (u k b)"),
                               z[(i // 2) % 2][:, i % 2].rearrange("p m b -> p (m b)"), ACT.Tanh).then_inc(tanh_done, 1)

            for i in range(GT):
                tanh(i, i)
            for i in range(GT):
                tanh(GT + i, i)
                gelu_chunk(act, 0, i, E, 512)
            with act.Fori(2, NG) as g:
                for i in range(GT):
                    tanh(g * GT + i, i)
                    gelu_chunk(act, g - 1, i, E, 512)
            for j in range(NCH):
                if j == 3:
                    act.wait_ge(nmax_done, 1)
                    act.activation(ex, logit, ACT.Exp, bias=nmax).then_inc(exp_done, 1)
                gelu_chunk(act, NG - 1, j, E, 512)
            act.wait_ge(lists_done, 3)
            sv = [act.value_load(starts[0:1, e:e + 1], min_val=0, max_val=MAXG) for e in range(E + 1)]
            for e in range(E):
                with act.Fori(sv[e], sv[e + 1]) as r:
                    g = r + NG
                    for j in range(NCH):
                        gelu_chunk(act, g, j, e, SLOTS * TOKS[e])

        @block.vector
        def _(dve):
            count = [0]

            def link(ins):
                count[0] += 1
                ins.then_inc(dve_math, 1)
                dve.wait_ge(dve_math, count[0])

            def split_lo(g, j, n):
                c = g * NCH + j
                dve.wait_ge(ghi_done, c + 1)
                dve.tensor_tensor(g_lo[:, j % 2, 0:n], g_f[:, j % 2, 0:n], g_hi[:, j % 2, 0:n].bitcast(F32),
                                  ALU.subtract).then_inc(glo_done, 1)

            def cell(s, i, first):
                dve.wait_ge(tanh_done, s + 1)
                dve.wait_ge(h_done, s + 1)
                dve.tensor_tensor(d_t[:], h_f[:, i % 2], uc[:, 1], ALU.subtract).then_inc(d_done, 1)
                dve.wait_ge(d_done, s + 1)
                dve.scalar_tensor_tensor(out=d_t[:], in0=uc[:, 0], scalar=1.0, in1=d_t[:],
                                         op0=ALU.add, op1=ALU.mult).then_inc(q_done, 1)
                dve.wait_ge(q_done, s + 1)
                dve.scalar_tensor_tensor(out=h_hi[:], in0=d_t[:], scalar=0.5, in1=uc[:, 1],
                                         op0=ALU.mult, op1=ALU.add).then_inc(hhi_done, 1)
                if not (first and i == 0):
                    dve.wait_ge(x1_sum, s)
                dve.scalar_tensor_tensor(out=h_f[:, 1 - i % 2], in0=d_t[:], scalar=0.5, in1=uc[:, 1],
                                         op0=ALU.mult, op1=ALU.add).then_inc(h_done, 1)
                dve.wait_ge(hhi_done, s + 2)
                dve.wait_ge(h_done, s + 2)
                dve.tensor_tensor(h_lo[:], h_f[:, 1 - i % 2], h_hi[:].bitcast(F32), ALU.subtract).then_inc(hlo_done, 1)

            def shared_out(g):
                dve.wait_ge(l2_done, (g + 1) * NCH)
                dve.wait_ge(x1_done, (g + 1) * GT)
                for k in range(K):
                    a = acc[:, k, bass.ds(g * GT, GT), :].rearrange("p t b -> p (t b)")
                    last = dve.scalar_tensor_tensor(out=a, in0=yp[0][k][:], scalar=par[:, S_B2 + E * K + k:S_B2 + E * K + k + 1],
                                                    in1=a, op0=ALU.add, op1=ALU.add)
                last.then_inc(y_read, 1)

            dve.memset(ones_r[:].bitcast(F32), 1.0).then_inc(ones_ready, 1)
            dve.wait_ge(s_w0, 32)
            for n in range(2 * K):
                src = (g_f if n < 2 else y_w)[:, n % 2]
                for a, scale in ((0, 0.5), (D, 1.0)):
                    link(dve.tensor_scalar(w0_hl[:, 0, n, a:a + D], src[:, a:a + D], scale, None, ALU.mult))
                    last = dve.scalar_tensor_tensor(out=w0_hl[:, 1, n, a:a + D], in0=src[:, a:a + D], scalar=scale,
                                                    in1=w0_hl[:, 0, n, a:a + D].bitcast(F32), op0=ALU.mult, op1=ALU.subtract)
            last.then_inc(w0_split, 1)
            dve.wait_ge(s_cond, 16)
            dve.tensor_copy(h_hi[:], h_f[:, 0]).then_inc(hhi_done, 1)
            dve.wait_ge(hhi_done, 1)
            dve.tensor_tensor(h_lo[:], h_f[:, 0], h_hi[:].bitcast(F32), ALU.subtract).then_inc(hlo_done, 1)
            dve.wait_ge(s_par, 48)
            dve.wait_ge(w0_split, 1)
            b_f, b_l = g_f[:, 0], g_f[:, 1]
            link(dve.tensor_scalar(b_f[:, 0:D], stage[:, 0, 0:D], 1.0, 0.5, ALU.add, ALU.mult))
            link(dve.tensor_copy(b_f[:, D:2 * D], stage[:, 0, D:2 * D]))
            link(dve.tensor_copy(bias0[:], b_f))
            link(dve.tensor_tensor(b_l, b_f, bias0[:].bitcast(F32), ALU.subtract))
            link(dve.tensor_scalar(b_l, b_l, con[:, C_M1:C_M1 + 1], None, ALU.mult))
            dve.scalar_tensor_tensor(out=bias0[:], in0=bias0[:].bitcast(F32), scalar=con[:, C_M0:C_M0 + 1], in1=b_l,
                                     op0=ALU.mult, op1=ALU.add).then_inc(bias_ready, 1)
            dve.wait_ge(bias_ready, 1)
            dve.wait_ge(silu_t, 1)
            link(dve.scalar_tensor_tensor(out=uc[:, 1], in0=uc[:, 0], scalar=1.0, in1=h_f[:, 0], op0=ALU.add, op1=ALU.mult))
            dve.tensor_scalar(d_t[:], uc[:, 1], 0.5, None, ALU.mult).then_inc(silu_done, 1)
            dve.sem_inc(h_done, 1)
            dve.wait_ge(mod_mm, 1)
            dve.tensor_tensor(mod_f, yp[1][0][0:B, 0:8], par[0:B, S_TB:S_TB + 8], ALU.add)

            for i in range(GT):
                cell(i, i, True)
            for i in range(GT):
                cell(GT + i, i, False)
                split_lo(0, i, 512)
            with dve.Fori(2, NG) as g:
                for i in range(GT):
                    cell(g * GT + i, i, False)
                    if i == 0:
                        pass
                    split_lo(g - 1, i, 512)
                    if i == 1:
                        shared_out(g - 2)

            def gate_means():
                dve.wait_ge(seg_done, T + 1)
                link(dve.tensor_tensor(agg[:, 1], seg[:, 0], seg[:, 2], ALU.add))
                link(dve.tensor_tensor(agg[:, 0], agg[:, 1], seg[:, 1], ALU.add))
                link(dve.tensor_tensor(agg[:, 2], seg[:, 1], seg[:, 2], ALU.add))
                link(dve.tensor_scalar(agg[:, 0], agg[:, 0], 1.0 / T, None, ALU.mult))
                dve.tensor_scalar(agg[:, 1:3], agg[:, 1:3], 1.0 / (HEAD + PROP), None, ALU.mult).then_inc(agg_done, 1)

            def gate_logits():
                dve.wait_ge(gate_mm, 1)
                link(dve.tensor_tensor(logit, z[0][0:B, 0, 0, 0:E], par[0:B, S_GB:S_GB + E], ALU.add))
                link(dve.scalar_tensor_tensor(out=logit, in0=mod_f[:, 0:E], scalar=1.0, in1=logit, op0=ALU.add, op1=ALU.mult))
                link(dve.tensor_tensor(logit, logit, mod_f[:, E:2 * E], ALU.add))
                link(dve.tensor_reduce(nmax, logit, AX_X, ALU.max))
                dve.tensor_scalar(nmax, nmax, -1.0, None, ALU.mult).then_inc(nmax_done, 1)

            def gate_choice():
                dve.wait_ge(exp_done, 1)
                link(dve.tensor_reduce(esum, ex, AX_X, ALU.add))
                link(dve.reciprocal(esum, esum))
                link(dve.tensor_scalar(score, ex, esum, None, ALU.mult))
                for j in range(E):
                    link(dve.tensor_scalar(rank4[:, j, 0:j + 1], score[:, 0:j + 1], score[:, j:j + 1], None, ALU.is_lt))
                    if j < E - 1:
                        link(dve.tensor_scalar(rank4[:, j, j + 1:E], score[:, j + 1:E], score[:, j:j + 1], None, ALU.is_le))
                link(dve.tensor_reduce(rank, rank4.rearrange("p j e -> p e j"), AX_X, ALU.add))
                dve.tensor_scalar(sel, rank, 1.5, None, ALU.is_lt).then_inc(sel_done, 1)
                dve.wait_ge(sel_done, 1)
                link(dve.tensor_tensor(wsel, sel, score, ALU.mult))
                link(dve.tensor_reduce(den, wsel, AX_X, ALU.add))
                link(dve.tensor_scalar(den, den, 1e-8, None, ALU.add))
                link(dve.reciprocal(den, den))
                link(dve.tensor_scalar(wsel, wsel, den, None, ALU.mult))

            def gate_slots():
                dve.wait_ge(pos_mm, 1)
                cnt = z[0][:, 0, 2, 0:E]
                link(dve.tensor_copy(ngr, cnt))
                link(dve.tensor_tensor(cmp8[:], ngr.unsqueeze(2).to_broadcast([P, E, SLOTS]),
                                       con[:, C_EIGHTS:C_EIGHTS + SLOTS].unsqueeze(1).to_broadcast([P, E, SLOTS]), ALU.is_gt))
                link(dve.tensor_reduce(ngr, cmp8[:], AX_X, ALU.add))
                link(dve.tensor_scalar(ngr, ngr, 1.0, None, ALU.max))
                link(dve.memset(start_f[:, 0:1], 0.0))
                for e in range(E):
                    link(dve.tensor_tensor(start_f[:, e + 1:e + 2], start_f[:, e:e + 1], ngr[:, e:e + 1], ALU.add))
                dve.tensor_copy(starts[:], start_f).then_inc(lists_done, 1)
                link(dve.tensor_scalar(gslot, start_f[0:B, 0:E], float(SLOTS), 4096.0, ALU.mult, ALU.add))
                link(dve.scalar_tensor_tensor(out=gslot, in0=sel, scalar=-4096.0, in1=gslot, op0=ALU.mult, op1=ALU.add))
                link(dve.tensor_tensor(gslot, gslot, z[0][0:B, 0, 1, 0:E], ALU.add))
                iota = con[0:B, C_IOTA:C_IOTA + NSLOT]
                link(dve.tensor_scalar(pick, iota, gslot[:, 0:1], None, ALU.is_equal))
                link(dve.tensor_scalar(pick_w, iota, gslot[:, 0:1], wsel[:, 0:1], ALU.is_equal, ALU.mult))
                for e in range(1, E):
                    link(dve.scalar_tensor_tensor(out=pick, in0=iota, scalar=gslot[:, e:e + 1], in1=pick,
                                                  op0=ALU.is_equal, op1=ALU.add))
                    link(dve.tensor_scalar(cmp_w, iota, gslot[:, e:e + 1], wsel[:, e:e + 1], ALU.is_equal, ALU.mult))
                    link(dve.tensor_tensor(pick_w, pick_w, cmp_w, ALU.add))
                dve.sem_inc(pick_done, 1)

            def gate_lists():
                dve.wait_ge(list_mm, 1)
                lists = z[1][:].rearrange("p a m b -> p (a m b)")
                dve.tensor_copy(slot_b[:], lists[0:1, 0:NSLOT]).then_inc(lists_done, 1)
                dve.tensor_copy(slot_w[:], lists[:, NSLOT:2 * NSLOT]).then_inc(lists_done, 1)

            gate_means()
            for j in range(NCH):
                split_lo(NG - 1, j, 512)
                if j == 1:
                    shared_out(NG - 2)
                    gate_logits()
                if j == 3:
                    gate_choice()
                if j == 5:
                    gate_slots()
            gate_lists()
            shared_out(NG - 1)
            dve.wait_ge(y_read, NG)
            dve.sem_inc(add_done, 1)

            dve.wait_ge(lists_done, 3)
            sv = [dve.value_load(starts[0:1, e:e + 1], min_val=0, max_val=MAXG) for e in range(E + 1)]
            for e in range(E):
                n = TOKS[e]
                with dve.Fori(sv[e], sv[e + 1]) as r:
                    g = r + NG
                    for j in range(NCH):
                        split_lo(g, j, SLOTS * n)
                    dve.wait_ge(l2_done, (g + 1) * NCH)
                    ws = slot_w[:, bass.ds(r * SLOTS, SLOTS)].unsqueeze(2).to_broadcast([P, SLOTS, n])
                    for k in range(K):
                        dve.scalar_tensor_tensor(
                            out=y_w[:, k, 0:SLOTS * n].rearrange("p (s n) -> p s n", n=n),
                            in0=yp[0][k][:, 0:SLOTS * n].rearrange("p (s n) -> p s n", n=n),
                            scalar=par[:, S_B2 + e * K + k:S_B2 + e * K + k + 1], in1=ws,
                            op0=ALU.add, op1=ALU.mult).then_inc(yw_done, 1)
                    dve.wait_ge(yw_done, (r + 1) * K)
                    dve.sem_inc(y_read, 1)
                    for s in range(SLOTS):
                        b = dve.value_load(slot_b[0:1, bass.ds(r * SLOTS + s, 1)], min_val=0, max_val=B - 1)
                        o = s * n
                        dve.wait_ge(add_done, r * SLOTS + s + 1)
                        for a, z_ in RUNS[e]:
                            dst = acc[:, :, a:z_, bass.ds(b, 1)].rearrange("p k t b -> p k (t b)")
                            last = dve.tensor_tensor(dst, dst, y_w[:, :, o:o + z_ - a], ALU.add)
                            o += z_ - a
                        last.then_inc(add_done, 1)
            dve.wait_ge(add_done, sv[E] * SLOTS + 1)
            dve.sem_inc(out_ready, 1)

        @block.tensor
        def _(pe):
            def mm(out_, lhsT, rhs, start, stop=False):
                return pe.matmul(out_, lhsT=lhsT, rhs=rhs, start=start, stop=stop, skip_group_check=True)

            def x_part(s, b):
                zz = z[b]
                for m in range(2 * K):
                    c = slice(m * P, (m + 1) * P)
                    o = zz[:, :, m, :]
                    mm(o, bias0[:, c], ones_r[:], m == 0)
                    for k in range(K):
                        hi = x_hl[:, 0, k, bass.ds(s, 2), :]
                        lo = x_hl[:, 1, k, bass.ds(s, 2), :]
                        mm(o, w0_hl[:, 0, k, c], hi, False)
                        mm(o, w0_hl[:, 1, k, c], hi, False)
                        mm(o, w0_hl[:, 0, k, c], lo, False)

            def h_part(s, i):
                o = z[(i // 2) % 2][:, i % 2]
                pe.wait_ge(hhi_done, s + 1)
                for m in range(2 * K):
                    c = slice(m * P, (m + 1) * P)
                    for k in range(K):
                        mm(o[:, m], w0_hl[:, 0, K + k, c], h_hi[:, k], False)
                        mm(o[:, m], w0_hl[:, 1, K + k, c], h_hi[:, k], False)
                pe.wait_ge(hlo_done, s + 1)
                for m in range(2 * K):
                    c = slice(m * P, (m + 1) * P)
                    for k in range(K):
                        last = mm(o[:, m], w0_hl[:, 0, K + k, c], h_lo[:, k], False, True)
                last.then_inc(z_done, 1)

            def layer1(g, j, w, src, n, first):
                c = g * NCH + j
                if not (isinstance(g, int) and g == 0 and j < 2):
                    pe.wait_ge(gelu_done, c - 1)
                for k in range(K):
                    o = k * HID + j * P
                    hi, lo = src(0, k), src(1, k)
                    mm(hp[j % 2][:, 0:n], w[:, 0, o:o + P], hi, k == 0)
                    mm(hp[j % 2][:, 0:n], w[:, 1, o:o + P], hi, False)
                    last = mm(hp[j % 2][:, 0:n], w[:, 0, o:o + P], lo, False, k == K - 1)
                last.then_inc(l1_done, 1)

            def layer2(g, j, w, n):
                c = g * NCH + j
                if j == 0 and not (isinstance(g, int) and g == 0):
                    pe.wait_ge(y_read, g)
                pe.wait_ge(ghi_done, c + 1)
                for m in range(K):
                    o = WCOLS + j * D + m * P
                    mm(yp[0][m][:, 0:n], w[:, 0, o:o + P], g_hi[:, j % 2, 0:n], j == 0)
                    mm(yp[0][m][:, 0:n], w[:, 1, o:o + P], g_hi[:, j % 2, 0:n], False)
                pe.wait_ge(glo_done, c + 1)
                for m in range(K):
                    o = WCOLS + j * D + m * P
                    last = mm(yp[0][m][:, 0:n], w[:, 0, o:o + P], g_lo[:, j % 2, 0:n], False, j == NCH - 1)
                last.then_inc(l2_done, 1)

            def group_src(g):
                return lambda part, k: x_hl[:, part, k, bass.ds(g * GT, GT), :]

            pe.wait_ge(silu_done, 1)
            pe.wait_ge(s_par, 48)
            for k in range(K):
                last = mm(yp[1][0][0:B, 0:2 * E], d_t[:, k], par[:, S_TW + 2 * E * k:S_TW + 2 * E * (k + 1)], k == 0, k == K - 1)
            last.then_inc(mod_mm, 1)
            pe.wait_ge(w0_split, 1)
            pe.wait_ge(bias_ready, 1)
            pe.wait_ge(ones_ready, 1)
            pe.wait_ge(xs_done, 2)
            x_part(0, 0)

            def steps(g, filler, carry, last_group=False):
                for i in range(GT):
                    s = g * GT + i
                    h_part(s, i)
                    if i % 2 == 0 and not (last_group and i == GT - 2):
                        if not (isinstance(g, int) and g == 0 and i < 2):
                            pe.wait_ge(tanh_done, s)
                        if not last_group:
                            pe.wait_ge(xs_done, s + 4)
                        x_part(s + 2, (i // 2 + 1) % 2)
                    if filler:
                        f = g - 1
                        if i == 0:
                            pe.wait_ge(x1_done, g * GT)
                        layer1(f, i, w_buf[0], group_src(f), 512, i == 0)
                        if i:
                            layer2(f, i - 1, w_buf[0], 512)
                        elif carry:
                            layer2(f - 1, NCH - 1, w_buf[0], 512)

            steps(0, False, False)
            pe.wait_ge(piece_done, NP)
            steps(1, True, False)
            with pe.Fori(2, NG - 1) as g:
                steps(g, True, True)
            steps(NG - 1, True, True, True)
            f = NG - 1
            pe.wait_ge(x1_done, T)
            for j in range(NCH):
                layer1(f, j, w_buf[0], group_src(f), 512, j == 0)
                if j:
                    layer2(f, j - 1, w_buf[0], 512)
                else:
                    layer2(f - 1, NCH - 1, w_buf[0], 512)
                if j == 1:
                    pe.wait_ge(agg_done, 1)
                    for i in range(3):
                        for k in range(K):
                            r = i * K + k
                            last = mm(z[0][0:B, 0, 0, 0:E], agg[:, i, k], par[:, S_GW + E * r:S_GW + E * (r + 1)],
                                      r == 0, r == 3 * K - 1)
                    last.then_inc(gate_mm, 1)
                if j == 5:
                    pe.wait_ge(sel_done, 1)
                    mm(z[0][:, 0, 2, 0:E], con[0:B, C_ONES:C_ONES + P], sel, True, True)
                    mm(z[0][0:B, 0, 1, 0:E], con[0:B, C_TRI:C_TRI + B], sel, False, True).then_inc(pos_mm, 1)
            layer2(f, NCH - 1, w_buf[0], 512)
            pe.wait_ge(pick_done, 1)
            lists = z[1][:].rearrange("p a m b -> p (a m b)")
            mm(lists[:, NSLOT:2 * NSLOT], con[0:B, C_ONES:C_ONES + P], pick_w, True, True)
            mm(lists[0:32, 0:NSLOT], con[0:B, C_BIDX:C_BIDX + 32], pick, False, True).then_inc(list_mm, 1)

            pe.wait_ge(lists_done, 3)
            sv = [pe.value_load(starts[0:1, e:e + 1], min_val=0, max_val=MAXG) for e in range(E + 1)]
            for e in range(E):
                n = SLOTS * TOKS[e]
                w = w_buf[(e + 1) % 2]
                pe.wait_ge(piece_done, (e + 2) * NP)
                with pe.Fori(sv[e], sv[e + 1]) as r:
                    g = r + NG
                    pe.wait_ge(gather_done, r + 2)
                    src = lambda part, k: xg[:, bass.ds(r % 2, 1), part, k, 0:n].rearrange("p i n -> p (i n)")
                    for j in range(NCH):
                        layer1(g, j, w, src, n, j == 0)
                        if j:
                            layer2(g, j - 1, w, n)
                    layer2(g, NCH - 1, w, n)


def kernel(**inputs):
    import numpy as np
    import concourse.bacc as bacc
    from concourse.bass_utils import run_bass_kernel_spmd

    def rows(a, n):
        a = np.asarray(a)
        return np.ascontiguousarray(a.reshape(n, P, -1).transpose(1, 0, 2).reshape(P, -1))

    g = {k: np.asarray(v) for k, v in inputs.items()}
    pre = "L1_cond_"
    x = g["x"].transpose(2, 1, 0).reshape(K, P, T, B).transpose(1, 0, 2, 3)
    cond = g["cond_1024"].T.reshape(K, P, B).transpose(1, 0, 2)
    w0 = rows(g["L0_cond_weight"], 2 * K)
    b0 = np.zeros((P, 2 * D), np.float32)
    b0[0:2] = g["L0_cond_bias"]
    w1 = list(g[pre + "ew1"]) + [g[pre + "sw1"]]
    w2 = list(g[pre + "ew2"]) + [g[pre + "sw2"]]
    w_exp = np.stack([np.concatenate([rows(a, K), rows(b, NCH)], axis=1) for a, b in zip(w1, w2)])
    b1 = np.concatenate([rows(a, NCH) for a in [*g[pre + "eb1"], g[pre + "sb1"]]], axis=1)
    b2 = np.concatenate([rows(a, K) for a in [*g[pre + "eb2"], g[pre + "sb2"]]], axis=1)
    small = np.concatenate([
        b1, b2, rows(g[pre + "gate_w"], 3 * K), rows(g[pre + "time_w"], K),
        np.broadcast_to(g[pre + "gate_b"], (P, E)), np.broadcast_to(g[pre + "time_b"], (P, 2 * E))], axis=1)
    consts = np.zeros((P, C_END), np.float32)
    consts[0:B, C_TRI:C_TRI + B] = np.triu(np.ones((B, B)), 1)
    consts[:, C_IOTA:C_IOTA + NSLOT] = np.arange(NSLOT)
    consts[:, C_BIDX:C_BIDX + 32] = np.arange(P)[:, None]
    consts[:, C_ONES:C_ONES + P] = 1
    consts[:, C_EIGHTS:C_EIGHTS + SLOTS] = SLOTS * np.arange(SLOTS)
    consts[0, C_M0] = 1
    consts[1, C_M1] = 1

    nc = bacc.Bacc("TRN2", target_bir_lowering=False, num_devices=1)
    arrays, args = {}, []
    for name, a in (("x", x), ("cond", cond), ("w0", w0), ("b0", b0), ("w_exp", w_exp), ("small", small), ("consts", consts)):
        a = np.ascontiguousarray(a)
        arrays[f"in_{name}"] = a
        args.append(nc.dram_tensor(f"in_{name}", a.shape, mybir.dt.from_np(a.dtype), kind="ExternalInput").ap())
    args.append(nc.dram_tensor("out_y", (P, K, T, B), F32, kind="ExternalOutput").ap())
    cond_resid_kernel(nc, *args)
    r = run_bass_kernel_spmd(nc, [arrays], core_ids=[0])
    y = r.results[0]["out_y"]
    return np.ascontiguousarray(y.transpose(3, 2, 1, 0).reshape(B, T, K * P))
```

```python
from contextlib import ExitStack

import concourse.bass as bass
from concourse import mybir

F32 = mybir.dt.float32
F32R = mybir.dt.float32r
BF16 = mybir.dt.bfloat16
I32 = mybir.dt.int32
ALU = mybir.AluOpType
ACT = mybir.ActivationFunctionType
AX_X = mybir.AxisListType.X

P = 128
B = 64
T = 64
D = 256
K = D // P
E = 4
HID = 1024
NCH = HID // P
GT = 8
NG = T // GT
QT = 4
SLOTS = 8
HEAD = T // 3
PROP = T - 2 * HEAD
MAXG = (2 * B + (SLOTS - 1) * E) // SLOTS + 1
NSLOT = MAXG * SLOTS
PIECE = 512
WCOLS = K * HID

ORDER = [E, 0, 3, 1, 2]
RUNS = [(0, 1, T, T), (0, 2, 2 * HEAD, PROP), (HEAD, 1, T, T - HEAD), (0, 1, T, T)]
TOKS = [n * length for _, n, _, length in RUNS]
MASKED_EXPERT, MASKED_STEP = 1, HEAD
assert PROP == HEAD + 1

C_TRI = 0
C_IOTA = C_TRI + B
C_BIDX = C_IOTA + NSLOT
C_ONES = C_BIDX + 32
C_EIGHTS = C_ONES + P
C_M0 = C_EIGHTS + SLOTS
C_M1 = C_M0 + 1
C_END = C_M1 + 1
S_B1, S_B2, S_GW, S_TW, S_GB, S_TB = 0, 40, 50, 74, 90, 94
S_END = 102


def cond_resid_kernel(nc, x, cond, w0, b0, w_exp, small, consts, out):
    ctx = ExitStack()
    with ctx:
        def sb(name, shape, dt=F32):
            return ctx.enter_context(nc.sbuf_tensor(name, shape, dt))

        def psum(name, shape):
            return ctx.enter_context(nc.psum_tensor(name, shape, F32))

        def sem(name):
            return ctx.enter_context(nc.semaphore(name))

        acc = sb("acc", [P, K, T, B])
        x_hl = sb("x_hl", [P, 2, K, T, B], F32R)
        w_buf = [sb(f"w_buf{i}", [P, 2, 2 * WCOLS], F32R) for i in range(2)]
        shared_buf = sb("shared_buf", [P, 4096], F32R)
        xg = shared_buf[:].rearrange("p (i s k n) -> p i s k n", i=2, s=2, k=K)
        wx = shared_buf[:, 0:2048].rearrange("p (s k n) -> p s k n", s=2, k=K)
        bias0 = shared_buf[:, 2048:2560]
        ones_r = shared_buf[:, 2560:2816]
        y_all = sb("y_all", [P, 1536])
        wh = y_all[:].bitcast(BF16).rearrange("p (i k n) -> p i k n", i=3, k=K)
        y_w = y_all[:, 0:1024].rearrange("p (k n) -> p k n", k=K)
        agg = y_all[:, 640:640 + 3 * K * B].rearrange("p (i k b) -> p i k b", i=3, k=K)
        pick = y_all[0:B, 0:NSLOT]
        pick_w = y_all[0:B, NSLOT:2 * NSLOT]
        raw_w0 = acc[:, 0, 32:64, :].rearrange("p t b -> p (t b)").rearrange("p (k n) -> p k n", n=2 * D)
        raw_b0 = acc[:, 1, 32:40, :].rearrange("p t b -> p (t b)")
        tmp_w0 = acc[:, 1, 40:48, :].rearrange("p t b -> p (t b)")
        stage = sb("stage", [P, 2, PIECE])
        g_f = sb("g_f", [P, 2, 512])
        g_hi = sb("g_hi", [P, 2, 512], F32R)
        g_lo = sb("g_lo", [P, 2, 512], F32R)
        uc = sb("uc", [P, 2, K, B])
        d_t = sb("d_t", [P, K, B])
        h_f = sb("h_f", [P, 2, K, B])
        h_r = sb("h_r", [P, K, B])
        h_b = sb("h_b", [P, 3, K, B], BF16)
        seg = sb("seg", [P, 3, K, B])
        par = sb("par", [P, S_END])
        con = sb("con", [P, C_END])
        slot_w = sb("slot_w", [P, NSLOT])
        turn = sb("turn", [P, 2])
        gs = sb("gs", [P, 96])
        cmp8 = sb("cmp8", [P, E, SLOTS])
        slot_b = sb("slot_b", [1, SLOTS + NSLOT], I32)
        starts = sb("starts", [P, E + 1], I32)

        zy = psum("zy", [P, 3 * K, 512])
        zb = zy[:, 0:4].rearrange("p (i a) (m t b) -> p i a m t b", i=2, m=2, t=QT)
        hp = [psum(f"hp{i}", [P, 512]) for i in range(2)]
        yp = [zy[:, 4 + k] for k in range(K)]
        gp, lists = zy[:, 0], zy[:, 1]

        mod_f = gs[0:B, 0:8]
        logit = gs[0:B, 8:12]
        nmax = gs[0:B, 12:13]
        ex = gs[0:B, 13:17]
        esum = gs[0:B, 17:18]
        score = gs[0:B, 18:22]
        rank4 = gs[0:B, 22:38].rearrange("p (j e) -> p j e", j=E)
        rank = gs[0:B, 38:42]
        sel = gs[0:B, 42:46]
        wsel = gs[0:B, 46:50]
        den = gs[0:B, 50:51]
        ngr = gs[:, 51:55]
        start_f = gs[:, 55:60]
        gslot = gs[0:B, 60:64]
        cmp_w = slot_w[0:B, :]

        s_cond, s_w0, s_b0, s_par, s_x0, s_x1, s_out = (
            sem(n) for n in ("s_cond", "s_w0", "s_b0", "s_par", "s_x0", "s_x1", "s_out"))
        piece_in = [sem(f"piece_in{i}") for i in range(2)]
        wx_hi, wx_split, wh_split, bias_ready, ones_ready = (
            sem(n) for n in ("wx_hi", "wx_split", "wh_split", "bias_ready", "ones_ready"))
        piece_hi, piece_done = sem("piece_hi"), sem("piece_done")
        x0_hi, x0_done, xs_hi, xs_done = (sem(n) for n in ("x0_hi", "x0_done", "xs_hi", "xs_done"))
        z_done, tanh_done, d_done, q_done, h_done = (sem(n) for n in ("z_done", "tanh_done", "d_done", "q_done", "h_done"))
        h1_done, hr_done, h2_done, h3_done = (sem(n) for n in ("h1_done", "hr_done", "h2_done", "h3_done"))
        x1_sum, x1_hi, x1_done, seg_done = (sem(n) for n in ("x1_sum", "x1_hi", "x1_done", "seg_done"))
        l1_done, l2_done, y_read = sem("l1_done"), sem("l2_done"), sem("y_read")
        gelu_done, ghi_done, glo_done = sem("gelu_done"), sem("ghi_done"), sem("glo_done")
        silu_t, silu_done, mod_mm = sem("silu_t"), sem("silu_done"), sem("mod_mm")
        agg_done, gate_mm, nmax_done, exp_done = sem("agg_done"), sem("gate_mm"), sem("nmax_done"), sem("exp_done")
        sel_done, pos_mm, pick_done, list_mm, lists_done = (
            sem(n) for n in ("sel_done", "pos_mm", "pick_done", "list_mm", "lists_done"))
        dve_math = sem("dve_math")
        gather_done, yw_done, add_done = sem("gather_done"), sem("yw_done"), sem("add_done")
        head_ready, out_ready = sem("head_ready"), sem("out_ready")

        NP = 2 * WCOLS // PIECE

        def w_of(i):
            return w_buf[i % 2]

        def group_bounds(eng):
            eng.wait_ge(lists_done, 3)
            return [eng.value_load(starts[0:1, e:e + 1], min_val=0, max_val=MAXG) for e in range(E + 1)]

        def y_bank(r):
            return [zy[:, bass.ds((r % 2) * K + 2 + k, 1), :].rearrange("p i n -> p (i n)") for k in range(K)]

        def pieces_at(j):
            return [[], [0], [1], [2], [3], [4], [5], [6, 7]][j]

        def tokens_of(t, e, b):
            first, n, step, length = RUNS[e]
            v = t[..., first:first + n * length, bass.ds(b, 1)]
            if len(v.shape) == 5:
                v = v.rearrange("p s k (i t) b -> p (s k) i (t b)", i=n)
            else:
                v = v.rearrange("p k (i t) b -> p k i (t b)", i=n)
            return bass.AP(v.tensor, v.offset, [list(v.ap[0]), list(v.ap[1]), [step * B, n], [B, length]])

        block = ctx.enter_context(nc.Block())

        @block.sync
        def _(sp):
            sp.dma_start(raw_w0[:, 0:K], w0[:, 0:K * 2 * D].rearrange("p (k n) -> p k n", k=K)).then_inc(s_w0, 16)
            sp.dma_start(acc[:, :, 0:GT], x[:, :, 0:GT]).then_inc(s_x0, 16)
            sp.dma_start(con[:], consts).then_inc(s_par, 16)
            sp.dma_start(par[:], small).then_inc(s_par, 16)
            for n in range(len(ORDER) * NP):
                if n == 2:
                    sp.wait_ge(wx_split, K)
                    sp.wait_ge(wh_split, K)
                    sp.wait_ge(bias_ready, 1)
                    sp.dma_start(acc[:, :, GT:T], x[:, :, GT:T]).then_inc(s_x1, 16)
                if n >= 2:
                    sp.wait_ge(piece_done, n - 1)
                e, j = ORDER[n // NP], n % NP
                sp.dma_start(stage[:, n % 2], w_exp[e, :, j * PIECE:(j + 1) * PIECE]).then_inc(piece_in[n % 2], 16)
            sp.wait_ge(head_ready, 1)
            sp.dma_start(out[:, :, 0:HEAD], acc[:, :, 0:HEAD]).then_inc(s_out, 16)
            sp.wait_ge(out_ready, 1)
            sp.dma_start(out[:, :, HEAD:T], acc[:, :, HEAD:T]).then_inc(s_out, 16)
            sp.wait_ge(s_out, 32)

        @block.gpsimd
        def _(pool):
            def split_x(s):
                pool.tensor_copy(x_hl[:, 0, :, bass.ds(s, 1), :], acc[:, :, bass.ds(s, 1), :]).then_inc(xs_hi, 1)
                pool.wait_ge(xs_hi, s - QT + 1)
                pool.tensor_tensor(x_hl[:, 1, :, bass.ds(s, 1), :], acc[:, :, bass.ds(s, 1), :],
                                   x_hl[:, 0, :, bass.ds(s, 1), :].bitcast(F32), ALU.subtract).then_inc(xs_done, 1)

            def add_h(s, i):
                a = acc[:, :, bass.ds(s, 1), :].rearrange("p k t b -> p k (t b)")
                hi = x_hl[:, 0, :, bass.ds(s, 1), :].rearrange("p k t b -> p k (t b)")
                lo = x_hl[:, 1, :, bass.ds(s, 1), :].rearrange("p k t b -> p k (t b)")
                sg = seg[:, bass.ds((s * 3 + 2) // 64, 1)].rearrange("p s k b -> p (s k) b")
                pool.wait_ge(h_done, s + 2)
                pool.tensor_tensor(hi, a, h_f[:, 1 - i % 2], ALU.add).then_inc(x1_hi, 1)
                pool.tensor_tensor(a, a, h_f[:, 1 - i % 2], ALU.add).then_inc(x1_sum, 1)
                pool.wait_ge(x1_sum, s + 1)
                pool.tensor_tensor(lo, a, hi.bitcast(F32), ALU.subtract).then_inc(x1_done, 1)
                pool.wait_ge(seg_done, s + 1)
                pool.tensor_tensor(sg, sg, a, ALU.add).then_inc(seg_done, 1)

            pool.memset(turn[:], 0.0).then_inc(gather_done, 1)
            pool.memset(seg[:], 0.0).then_inc(seg_done, 1)
            pool.wait_ge(s_x0, 16)
            for s in range(QT, GT):
                split_x(s)
            for s in range(GT):
                add_h(s, s)
                if s == 0:
                    pool.wait_ge(s_x1, 16)
                split_x(s + GT)
            with pool.Fori(1, NG - 1) as g:
                for i in range(GT):
                    add_h(g * GT + i, i)
                    split_x(g * GT + GT + i)
            for i in range(GT):
                add_h((NG - 1) * GT + i, i)

            sv = group_bounds(pool)
            for q in range(E):
                e = ORDER[q + 1]
                n = TOKS[e]
                with pool.Fori(sv[q], sv[q + 1]) as r:
                    bs = nc.values_load_multi_w_load_instructions(slot_b[0:1, bass.ds(r * SLOTS + SLOTS, SLOTS)], engines=(mybir.EngineType.Pool,), min_val=0, max_val=B - 1)[1]
                    pool.wait_ge(l1_done, (r + NG - 1) * NCH)
                    pool.wait_ge(gather_done, r + 1)
                    pool.tensor_tensor(turn[:, 1:2], turn[:, 0:1], turn[:, 0:1], ALU.mult)
                    for s in range(SLOTS):
                        dst = xg[:, bass.ds(r % 2, 1), :, :, s * n:(s + 1) * n].rearrange(
                            "p i s k (a n) -> p (i s k) a n", a=RUNS[e][1])
                        last = pool.tensor_copy(dst, tokens_of(x_hl, e, bs[s]))
                    last.then_inc(gather_done, 1)

        @block.scalar
        def _(act):
            def tanh(s, i, buf):
                act.wait_ge(z_done, s + 1)
                act.activation(uc[:],
                               zb[:, buf, :, :, i % QT, :], ACT.Tanh).then_inc(tanh_done, 1)

            def gelu_chunk(g, j, e, n, very_first=False):
                c = g * NCH + j
                act.wait_ge(l1_done, c + 1)
                if not very_first:
                    act.wait_ge(glo_done, c - 1)
                act.activation(g_f[:, j % 2, 0:n], hp[j % 2][:, 0:n], ACT.Gelu_apprx_tanh,
                               bias=par[:, S_B1 + e * NCH + j:S_B1 + e * NCH + j + 1]).then_inc(gelu_done, 1)
                act.wait_ge(gelu_done, c + 1)
                if not very_first:
                    act.wait_ge(l2_done, c - 1)
                act.activation(g_hi[:, j % 2, 0:n], g_f[:, j % 2, 0:n], ACT.Copy).then_inc(ghi_done, 1)

            def piece_high(n):
                c = n % NP * PIECE
                act.wait_ge(piece_in[n % 2], 16 * (n // 2 + 1))
                act.activation(w_of(n // NP)[:, 0, c:c + PIECE], stage[:, n % 2], ACT.Copy).then_inc(piece_hi, 1)

            act.dma_start(h_f[:, 0], cond).then_inc(s_cond, 16)
            act.dma_start(raw_w0[:, K:2 * K], w0[:, K * 2 * D:2 * K * 2 * D].rearrange("p (k n) -> p k n", k=K)).then_inc(s_w0, 16)
            act.dma_start(raw_b0, b0).then_inc(s_b0, 16)
            act.wait_ge(ones_ready, 1)
            act.activation(gs[:, 64:65], ones_r[:, 0:1].bitcast(F32), ACT.Gelu_apprx_tanh)
            act.wait_ge(s_cond, 16)
            act.activation(uc[:, 0], h_f[:, 0], ACT.Tanh, scale=0.5).then_inc(silu_t, 1)
            act.wait_ge(s_w0, 32)
            for k in range(K):
                act.activation(wx[:, 0, k, 0:D], raw_w0[:, k, 0:D], ACT.Copy, scale=0.5)
                act.activation(wx[:, 0, k, D:2 * D], raw_w0[:, k, D:2 * D], ACT.Copy).then_inc(wx_hi, 1)
            act.wait_ge(s_x0, 16)
            act.activation(x_hl[:, 0, :, 0:QT], acc[:, :, 0:QT], ACT.Copy).then_inc(x0_hi, 1)

            for i in range(GT):
                tanh(i, i, i // QT)
                piece_high(i)
            for i in range(GT):
                tanh(GT + i, i, i // QT)
                gelu_chunk(0, i, E, 512, i < 2)
                piece_high(NP + i)
            with act.Fori(2, NG) as g:
                for i in range(GT):
                    tanh(g * GT + i, i, i // QT)
                    gelu_chunk(g - 1, i, E, 512)
            for j in range(NCH):
                if j == 3:
                    act.wait_ge(nmax_done, 1)
                    act.activation(ex, logit, ACT.Exp, bias=nmax).then_inc(exp_done, 1)
                gelu_chunk(NG - 1, j, E, 512)
            sv = group_bounds(act)
            for q in range(E):
                e = ORDER[q + 1]
                n = SLOTS * TOKS[e]
                with act.Fori(sv[q], sv[q + 1]) as r:
                    if q < E - 1:
                        with act.If(sv[q] < r):
                            for j in range(NCH):
                                gelu_chunk(r + NG, j, e, n)
                        with act.Else():
                            for j in range(NCH):
                                gelu_chunk(r + NG, j, e, n)
                                if pieces_at(j) == [0]:
                                    act.wait_ge(l2_done, (r + NG) * NCH)
                                for m in pieces_at(j):
                                    piece_high((q + 2) * NP + m)
                    else:
                        for j in range(NCH):
                            gelu_chunk(r + NG, j, e, n)

        @block.vector
        def _(dve):
            count = [0]

            def link(ins):
                count[0] += 1
                ins.then_inc(dve_math, 1)
                dve.wait_ge(dve_math, count[0])

            def split_lo(g, j, n):
                c = g * NCH + j
                dve.wait_ge(ghi_done, c + 1)
                dve.tensor_tensor(g_lo[:, j % 2, 0:n], g_f[:, j % 2, 0:n], g_hi[:, j % 2, 0:n].bitcast(F32),
                                  ALU.subtract).then_inc(glo_done, 1)

            def piece_low(n):
                w = w_of(n // NP)
                c = n % NP * PIECE
                dve.wait_ge(piece_hi, n + 1)
                dve.tensor_tensor(w[:, 1, c:c + PIECE], stage[:, n % 2], w[:, 0, c:c + PIECE].bitcast(F32),
                                  ALU.subtract).then_inc(piece_done, 1)

            def split_state(s, h):
                dve.wait_ge(h1_done, s + 2)
                dve.wait_ge(h_done, s + 2)
                dve.tensor_tensor(h_r[:], h, h_b[:, 0], ALU.subtract).then_inc(hr_done, 1)
                dve.wait_ge(hr_done, s + 2)
                dve.tensor_copy(h_b[:, 1], h_r[:]).then_inc(h2_done, 1)
                dve.wait_ge(h2_done, s + 2)
                dve.tensor_tensor(h_b[:, 2], h_r[:], h_b[:, 1], ALU.subtract).then_inc(h3_done, 1)

            def cell(s, i, first=False):
                dve.wait_ge(tanh_done, s + 1)
                dve.wait_ge(h_done, s + 1)
                dve.tensor_tensor(d_t[:], h_f[:, i % 2], uc[:, 1], ALU.subtract).then_inc(d_done, 1)
                dve.wait_ge(d_done, s + 1)
                dve.scalar_tensor_tensor(out=d_t[:], in0=uc[:, 0], scalar=1.0, in1=d_t[:],
                                         op0=ALU.add, op1=ALU.mult).then_inc(q_done, 1)
                dve.wait_ge(q_done, s + 1)
                dve.scalar_tensor_tensor(out=h_b[:, 0], in0=d_t[:], scalar=0.5, in1=uc[:, 1],
                                         op0=ALU.mult, op1=ALU.add).then_inc(h1_done, 1)
                if not first:
                    dve.wait_ge(x1_sum, s)
                dve.scalar_tensor_tensor(out=h_f[:, 1 - i % 2], in0=d_t[:], scalar=0.5, in1=uc[:, 1],
                                         op0=ALU.mult, op1=ALU.add).then_inc(h_done, 1)
                split_state(s, h_f[:, 1 - i % 2])

            def shared_out(g):
                dve.wait_ge(l2_done, (g + 1) * NCH)
                dve.wait_ge(x1_done, (g + 1) * GT)
                for k in range(K):
                    a = acc[:, k, bass.ds(g * GT, GT), :].rearrange("p t b -> p (t b)")
                    last = dve.scalar_tensor_tensor(out=a, in0=yp[k], scalar=par[:, S_B2 + E * K + k:S_B2 + E * K + k + 1],
                                                    in1=a, op0=ALU.add, op1=ALU.add)
                last.then_inc(y_read, 1)

            dve.memset(ones_r.bitcast(F32), 1.0).then_inc(ones_ready, 1)
            dve.wait_ge(s_cond, 16)
            dve.tensor_copy(h_b[:, 0], h_f[:, 0]).then_inc(h1_done, 1)
            dve.sem_inc(h_done, 1)
            split_state(-1, h_f[:, 0])
            for k in range(K):
                dve.wait_ge(wx_hi, k + 1)
                for a, scale in ((0, 0.5), (D, 1.0)):
                    last = dve.scalar_tensor_tensor(out=wx[:, 1, k, a:a + D], in0=raw_w0[:, k, a:a + D], scalar=scale,
                                                    in1=wx[:, 0, k, a:a + D].bitcast(F32), op0=ALU.mult, op1=ALU.subtract)
                last.then_inc(wx_split, 1)
            dve.wait_ge(s_b0, 16)
            dve.wait_ge(s_par, 32)
            link(dve.tensor_scalar(raw_b0[:, 0:D], raw_b0[:, 0:D], 1.0, 0.5, ALU.add, ALU.mult))
            link(dve.tensor_copy(bias0, raw_b0))
            link(dve.tensor_tensor(raw_b0, raw_b0, bias0.bitcast(F32), ALU.subtract))
            link(dve.tensor_scalar(raw_b0, raw_b0, con[:, C_M1:C_M1 + 1], None, ALU.mult))
            dve.scalar_tensor_tensor(out=bias0, in0=bias0.bitcast(F32), scalar=con[:, C_M0:C_M0 + 1], in1=raw_b0,
                                     op0=ALU.mult, op1=ALU.add).then_inc(bias_ready, 1)
            dve.wait_ge(x0_hi, 1)
            dve.tensor_tensor(x_hl[:, 1, :, 0:QT].rearrange("p k t b -> p k (t b)"),
                              acc[:, :, 0:QT].rearrange("p k t b -> p k (t b)"),
                              x_hl[:, 0, :, 0:QT].rearrange("p k t b -> p k (t b)").bitcast(F32), ALU.subtract).then_inc(x0_done, 1)
            for k in range(K):
                raw = raw_w0[:, K + k]
                link(dve.tensor_scalar(raw[:, 0:D], raw[:, 0:D], 0.5, None, ALU.mult))
                link(dve.tensor_copy(wh[:, 0, k], raw))
                link(dve.tensor_tensor(tmp_w0, raw, wh[:, 0, k], ALU.subtract))
                link(dve.tensor_copy(wh[:, 1, k], tmp_w0))
                dve.tensor_tensor(wh[:, 2, k], tmp_w0, wh[:, 1, k], ALU.subtract).then_inc(wh_split, 1)
            dve.wait_ge(silu_t, 1)
            link(dve.scalar_tensor_tensor(out=uc[:, 1], in0=uc[:, 0], scalar=1.0, in1=h_f[:, 0], op0=ALU.add, op1=ALU.mult))
            dve.tensor_scalar(d_t[:], uc[:, 1], 0.5, None, ALU.mult).then_inc(silu_done, 1)
            dve.wait_ge(mod_mm, 1)
            dve.tensor_tensor(mod_f, hp[0][0:B, 0:8], par[0:B, S_TB:S_TB + 8], ALU.add)

            for i in range(GT):
                cell(i, i, i == 0)
                piece_low(i)
            for i in range(GT):
                cell(GT + i, i)
                split_lo(0, i, 512)
                piece_low(NP + i)
            with dve.Fori(2, NG) as g:
                for i in range(GT):
                    if i == 2:
                        shared_out(g - 2)
                    cell(g * GT + i, i)
                    split_lo(g - 1, i, 512)

            def gate_means():
                dve.wait_ge(seg_done, T + 1)
                link(dve.tensor_tensor(agg[:, 1], seg[:, 0], seg[:, 2], ALU.add))
                link(dve.tensor_tensor(agg[:, 0], agg[:, 1], seg[:, 1], ALU.add))
                link(dve.tensor_tensor(agg[:, 2], seg[:, 1], seg[:, 2], ALU.add))
                link(dve.tensor_scalar(agg[:, 0], agg[:, 0], 1.0 / T, None, ALU.mult))
                dve.tensor_scalar(agg[:, 1:3], agg[:, 1:3], 1.0 / (HEAD + PROP), None, ALU.mult).then_inc(agg_done, 1)

            def gate_logits():
                dve.wait_ge(gate_mm, 1)
                link(dve.tensor_tensor(logit, gp[0:B, 0:E], par[0:B, S_GB:S_GB + E], ALU.add))
                link(dve.scalar_tensor_tensor(out=logit, in0=mod_f[:, 0:E], scalar=1.0, in1=logit, op0=ALU.add, op1=ALU.mult))
                link(dve.tensor_tensor(logit, logit, mod_f[:, E:2 * E], ALU.add))
                link(dve.tensor_reduce(nmax, logit, AX_X, ALU.max))
                dve.tensor_scalar(nmax, nmax, -1.0, None, ALU.mult).then_inc(nmax_done, 1)

            def gate_choice():
                dve.wait_ge(exp_done, 1)
                link(dve.tensor_reduce(esum, ex, AX_X, ALU.add))
                link(dve.reciprocal(esum, esum))
                link(dve.tensor_scalar(score, ex, esum, None, ALU.mult))
                for j in range(E):
                    link(dve.tensor_scalar(rank4[:, j, 0:j + 1], score[:, 0:j + 1], score[:, j:j + 1], None, ALU.is_lt))
                    if j < E - 1:
                        link(dve.tensor_scalar(rank4[:, j, j + 1:E], score[:, j + 1:E], score[:, j:j + 1], None, ALU.is_le))
                link(dve.tensor_reduce(rank, rank4.rearrange("p j e -> p e j"), AX_X, ALU.add))
                dve.tensor_scalar(sel, rank, 1.5, None, ALU.is_lt).then_inc(sel_done, 1)
                dve.wait_ge(sel_done, 1)
                link(dve.tensor_tensor(wsel, sel, score, ALU.mult))
                link(dve.tensor_reduce(den, wsel, AX_X, ALU.add))
                link(dve.tensor_scalar(den, den, 1e-8, None, ALU.add))
                link(dve.reciprocal(den, den))
                link(dve.tensor_scalar(wsel, wsel, den, None, ALU.mult))

            def gate_slots():
                dve.wait_ge(pos_mm, 1)
                link(dve.tensor_copy(ngr, gp[:, 2 * E:3 * E]))
                link(dve.tensor_tensor(cmp8[:], ngr.unsqueeze(2).to_broadcast([P, E, SLOTS]),
                                       con[:, C_EIGHTS:C_EIGHTS + SLOTS].unsqueeze(1).to_broadcast([P, E, SLOTS]), ALU.is_gt))
                link(dve.tensor_reduce(ngr, cmp8[:], AX_X, ALU.add))
                link(dve.tensor_scalar(ngr, ngr, 1.0, None, ALU.max))
                link(dve.memset(start_f[:, 0:1], 0.0))
                for q in range(E):
                    e = ORDER[q + 1]
                    link(dve.tensor_tensor(start_f[:, q + 1:q + 2], start_f[:, q:q + 1], ngr[:, e:e + 1], ALU.add))
                dve.tensor_copy(starts[:], start_f).then_inc(lists_done, 1)
                for q in range(E):
                    e = ORDER[q + 1]
                    link(dve.tensor_scalar(gslot[:, e:e + 1], start_f[0:B, q:q + 1], float(SLOTS), 4096.0, ALU.mult, ALU.add))
                link(dve.scalar_tensor_tensor(out=gslot, in0=sel, scalar=-4096.0, in1=gslot, op0=ALU.mult, op1=ALU.add))
                link(dve.tensor_tensor(gslot, gslot, gp[0:B, E:2 * E], ALU.add))
                iota = con[0:B, C_IOTA:C_IOTA + NSLOT]
                link(dve.tensor_scalar(pick, iota, gslot[:, 0:1], None, ALU.is_equal))
                link(dve.tensor_scalar(pick_w, iota, gslot[:, 0:1], wsel[:, 0:1], ALU.is_equal, ALU.mult))
                for e in range(1, E):
                    link(dve.scalar_tensor_tensor(out=pick, in0=iota, scalar=gslot[:, e:e + 1], in1=pick,
                                                  op0=ALU.is_equal, op1=ALU.add))
                    link(dve.tensor_scalar(cmp_w, iota, gslot[:, e:e + 1], wsel[:, e:e + 1], ALU.is_equal, ALU.mult))
                    link(dve.tensor_tensor(pick_w, pick_w, cmp_w, ALU.add))
                dve.sem_inc(pick_done, 1)

            def gate_lists():
                dve.wait_ge(list_mm, 1)
                dve.tensor_copy(slot_b[0:1, SLOTS:SLOTS + NSLOT], lists[0:1, 0:NSLOT]).then_inc(lists_done, 1)
                dve.tensor_copy(slot_w[:], lists[:, NSLOT:2 * NSLOT]).then_inc(lists_done, 1)

            gate_means()
            for j in range(NCH):
                if j == 2:
                    shared_out(NG - 2)
                split_lo(NG - 1, j, 512)
                if j == 1:
                    gate_logits()
                if j == 3:
                    gate_choice()
                if j == 4:
                    gate_slots()
            gate_lists()

            def weigh(r, e):
                n = TOKS[e]
                dve.wait_ge(l2_done, (r + NG + 1) * NCH)
                dve.wait_ge(add_done, (r + 1) * SLOTS + 1)
                ws = slot_w[:, bass.ds(r * SLOTS, SLOTS)].unsqueeze(2).to_broadcast([P, SLOTS, n])
                for k in range(K):
                    dve.scalar_tensor_tensor(
                        out=y_w[:, k, 0:SLOTS * n].rearrange("p (s n) -> p s n", n=n),
                        in0=y_bank(r)[k][:, 0:SLOTS * n].rearrange("p (s n) -> p s n", n=n),
                        scalar=par[:, S_B2 + e * K + k:S_B2 + e * K + k + 1], in1=ws,
                        op0=ALU.add, op1=ALU.mult).then_inc(yw_done, 1)
                dve.wait_ge(yw_done, (r + 1) * K)
                if e == MASKED_EXPERT:
                    dve.memset(y_w[:, :, 0:SLOTS * n].rearrange("p k (s n) -> p k s n", n=n)[:, :, :, MASKED_STEP],
                               0.0).then_inc(y_read, 1)
                else:
                    dve.sem_inc(y_read, 1)

            def add_slots(r, e, slots):
                n = TOKS[e]
                bs = nc.values_load_multi_w_load_instructions(slot_b[0:1, bass.ds(r * SLOTS + slots[0], len(slots))], engines=(mybir.EngineType.DVE,), min_val=0, max_val=B - 1)[1]
                for s, b in zip(slots, bs):
                    if s == 0:
                        dve.wait_ge(y_read, r + NG)
                    dve.wait_ge(add_done, r * SLOTS + s + 1)
                    dst = tokens_of(acc, e, b)
                    dve.tensor_tensor(dst, dst, y_w[:, :, s * n:(s + 1) * n].rearrange("p k (a n) -> p k a n", a=RUNS[e][1]),
                                      ALU.add).then_inc(add_done, 1)

            sv = group_bounds(dve)
            n0 = SLOTS * TOKS[ORDER[1]]
            split_lo(NG, 0, n0)
            shared_out(NG - 1)
            dve.wait_ge(y_read, NG)
            dve.sem_inc(add_done, SLOTS + 1)
            split_lo(NG, 1, n0)
            for q in range(E):
                e = ORDER[q + 1]
                n = SLOTS * TOKS[e]
                with dve.Fori(sv[q], sv[q + 1]) as r:
                    with dve.If(sv[q] < r):
                        for j in range(2, NCH):
                            split_lo(r + NG, j, n)
                            if j < 2 + SLOTS // 2:
                                add_slots(r, e, [2 * j - 4, 2 * j - 3])
                    with dve.Else():
                        for j in range(2, NCH):
                            split_lo(r + NG, j, n)
                            if q and 3 <= j < 3 + SLOTS // 2:
                                add_slots(r, ORDER[q], [2 * j - 6, 2 * j - 5])
                            if q < E - 1:
                                for m in (pieces_at(1) if j == 2 else []) + pieces_at(j):
                                    piece_low((q + 2) * NP + m)
                        if q == E - 1:
                            dve.wait_ge(add_done, (r + 1) * SLOTS + 1)
                            dve.sem_inc(head_ready, 1)
                    with dve.If(r + 1 < sv[q + 1]):
                        split_lo(r + NG + 1, 0, n)
                        weigh(r, e)
                        split_lo(r + NG + 1, 1, n)
                    with dve.Else():
                        nn = SLOTS * TOKS[ORDER[q + 2]] if q < E - 1 else 0
                        if nn:
                            split_lo(r + NG + 1, 0, nn)
                        weigh(r, e)
                        if nn:
                            split_lo(r + NG + 1, 1, nn)
            for s in range(0, SLOTS, 2):
                add_slots(sv[E], ORDER[E], [s, s + 1])
            dve.wait_ge(add_done, (sv[E] + 1) * SLOTS + 1)
            dve.sem_inc(out_ready, 1)

        @block.tensor
        def _(pe):
            def mm(out_, lhsT, rhs, start, stop=False):
                return pe.matmul(out_, lhsT=lhsT, rhs=rhs, start=start, stop=stop, skip_group_check=True)

            def x_part(s, buf, m):
                c = slice(m * P, (m + 1) * P)
                o = zb[:, buf, m // 2, m % 2].rearrange("p t b -> p (t b)")
                mm(o, bias0[:, c], ones_r, m % 2 == 0)
                for k in range(K):
                    hi = x_hl[:, 0, k, bass.ds(s, QT), :]
                    lo = x_hl[:, 1, k, bass.ds(s, QT), :]
                    mm(o, wx[:, 0, k, c], hi, False)
                    mm(o, wx[:, 1, k, c], hi, False)
                    mm(o, wx[:, 0, k, c], lo, False)

            def h_part(s, i, buf):
                for a, ready in enumerate((h1_done, h2_done, h3_done)):
                    pe.wait_ge(ready, s + 1)
                    for m in range(2 * K):
                        o = zb[:, buf, m // 2, m % 2, i % QT, :]
                        for k in range(K):
                            for b in range(3 - a):
                                last = mm(o, wh[:, b, k, m * P:(m + 1) * P], h_b[:, a, k], False, a == 2)
                last.then_inc(z_done, 1)

            def layer1(g, j, w, src, n, very_first=False):
                c = g * NCH + j
                if not very_first:
                    pe.wait_ge(gelu_done, c - 1)
                for k in range(K):
                    o = k * HID + j * P
                    hi, lo = src(0, k), src(1, k)
                    mm(hp[j % 2][:, 0:n], w[:, 0, o:o + P], hi, k == 0)
                    mm(hp[j % 2][:, 0:n], w[:, 1, o:o + P], hi, False)
                    last = mm(hp[j % 2][:, 0:n], w[:, 0, o:o + P], lo, False, k == K - 1)
                last.then_inc(l1_done, 1)

            def layer2(g, j, w, y, n):
                c = g * NCH + j
                pe.wait_ge(ghi_done, c + 1)
                for m in range(K):
                    o = WCOLS + j * D + m * P
                    mm(y[m][:, 0:n], w[:, 0, o:o + P], g_hi[:, j % 2, 0:n], j == 0)
                    mm(y[m][:, 0:n], w[:, 1, o:o + P], g_hi[:, j % 2, 0:n], False)
                pe.wait_ge(glo_done, c + 1)
                for m in range(K):
                    o = WCOLS + j * D + m * P
                    last = mm(y[m][:, 0:n], w[:, 0, o:o + P], g_lo[:, j % 2, 0:n], False, j == NCH - 1)
                last.then_inc(l2_done, 1)

            def group_src(g):
                return lambda part, k: x_hl[:, part, k, bass.ds(g * GT, GT), :]

            y0 = yp

            pe.wait_ge(silu_done, 1)
            pe.wait_ge(s_par, 32)
            for k in range(K):
                last = mm(hp[0][0:B, 0:2 * E], d_t[:, k], par[:, S_TW + 2 * E * k:S_TW + 2 * E * (k + 1)], k == 0, k == K - 1)
            last.then_inc(mod_mm, 1)
            pe.wait_ge(wx_split, K)
            pe.wait_ge(bias_ready, 1)
            pe.wait_ge(x0_done, 1)
            for m in range(2 * K):
                x_part(0, 0, m)
            pe.wait_ge(wh_split, K)

            def steps(g, filler, carry, last_group=False):
                for i in range(GT):
                    s = g * GT + i
                    h_part(s, i, i // QT)
                    if not (last_group and i >= QT):
                        if i % QT == 0:
                            if not (isinstance(g, int) and g == 0 and i == 0):
                                pe.wait_ge(tanh_done, s)
                            pe.wait_ge(xs_done, s + QT)
                        x_part(s - i % QT + QT, (i // QT + 1) % 2, i % QT)
                    if filler:
                        f = g - 1
                        if i == 0:
                            pe.wait_ge(x1_done, g * GT)
                        layer1(f, i, w_of(0), group_src(f), 512, not carry and i < 2)
                        if i == 2 and carry:
                            pe.wait_ge(y_read, f)
                        if i >= 2:
                            layer2(f, i - 2, w_of(0), y0, 512)
                        elif carry:
                            layer2(f - 1, NCH - 2 + i, w_of(0), y0, 512)

            steps(0, False, False)
            pe.wait_ge(piece_done, NP)
            steps(1, True, False)
            with pe.Fori(2, NG - 1) as g:
                steps(g, True, True)
            steps(NG - 1, True, True, True)
            f = NG - 1
            pe.wait_ge(x1_done, T)
            for j in range(NCH):
                layer1(f, j, w_of(0), group_src(f), 512)
                if j == 2:
                    pe.wait_ge(y_read, f)
                layer2(f if j >= 2 else f - 1, (j - 2) % NCH, w_of(0), y0, 512)
                if j == 1:
                    pe.wait_ge(agg_done, 1)
                    for i in range(3):
                        for k in range(K):
                            a = i * K + k
                            last = mm(gp[0:B, 0:E], agg[:, i, k], par[:, S_GW + E * a:S_GW + E * (a + 1)],
                                      a == 0, a == 3 * K - 1)
                    last.then_inc(gate_mm, 1)
                if j == 5:
                    pe.wait_ge(sel_done, 1)
                    mm(gp[:, 2 * E:3 * E], con[0:B, C_ONES:C_ONES + P], sel, True, True)
                    mm(gp[0:B, E:2 * E], con[0:B, C_TRI:C_TRI + B], sel, False, True).then_inc(pos_mm, 1)
            pe.wait_ge(pick_done, 1)
            mm(lists[:, NSLOT:2 * NSLOT], con[0:B, C_ONES:C_ONES + P], pick_w, True, True)
            mm(lists[0:32, 0:NSLOT], con[0:B, C_BIDX:C_BIDX + 32], pick, False, True).then_inc(list_mm, 1)

            sv = group_bounds(pe)

            def src_of(r, n):
                return lambda part, k: xg[:, bass.ds(r % 2, 1), part, k, 0:n].rearrange("p i n -> p (i n)")

            def turnover(r, i, n, w, y, r2, n2, w2):
                if n2:
                    pe.wait_ge(piece_done, i * NP + NP // 2)
                    pe.wait_ge(gather_done, r2 + 2)
                for j in range(2):
                    if n2:
                        layer1(r2 + NG, j, w2, src_of(r2, n2), n2)
                    layer2(r + NG, NCH - 2 + j, w, y, n)

            n0 = SLOTS * TOKS[ORDER[1]]
            turnover(-1, 1, 512, w_of(0), y0, 0, n0, w_of(1))
            for q in range(E):
                n = SLOTS * TOKS[ORDER[q + 1]]
                w = w_of(q + 1)
                with pe.Fori(sv[q], sv[q + 1]) as r:
                    y = y_bank(r)
                    for j in range(2, NCH):
                        layer1(r + NG, j, w, src_of(r, n), n)
                        if j == 2:
                            pe.wait_ge(y_read, r + NG - 1)
                            pe.wait_ge(piece_done, (q + 2) * NP)
                        layer2(r + NG, j - 2, w, y, n)
                    with pe.If(r + 1 < sv[q + 1]):
                        turnover(r, q + 1, n, w, y, r + 1, n, w)
                    with pe.Else():
                        if q < E - 1:
                            turnover(r, q + 2, n, w, y, r + 1, SLOTS * TOKS[ORDER[q + 2]], w_of(q + 2))
                        else:
                            turnover(r, 0, n, w, y, r + 1, 0, None)



def kernel(**inputs):
    import numpy as np
    import concourse.bacc as bacc
    from concourse.bass_utils import run_bass_kernel_spmd

    def rows(a, n):
        a = np.asarray(a)
        return np.ascontiguousarray(a.reshape(n, P, -1).transpose(1, 0, 2).reshape(P, -1))

    g = {k: np.asarray(v) for k, v in inputs.items()}
    pre = "L1_cond_"
    x = g["x"].transpose(2, 1, 0).reshape(K, P, T, B).transpose(1, 0, 2, 3)
    cond = g["cond_1024"].T.reshape(K, P, B).transpose(1, 0, 2)
    w0 = rows(g["L0_cond_weight"], 2 * K)
    b0 = np.zeros((P, 2 * D), np.float32)
    b0[0:2] = g["L0_cond_bias"]
    w1 = list(g[pre + "ew1"]) + [g[pre + "sw1"]]
    w2 = list(g[pre + "ew2"]) + [g[pre + "sw2"]]
    w_exp = np.stack([np.concatenate([rows(a, K), rows(b, NCH)], axis=1) for a, b in zip(w1, w2)])
    b1 = np.concatenate([rows(a, NCH) for a in [*g[pre + "eb1"], g[pre + "sb1"]]], axis=1)
    b2 = np.concatenate([rows(a, K) for a in [*g[pre + "eb2"], g[pre + "sb2"]]], axis=1)
    small = np.concatenate([
        b1, b2, rows(g[pre + "gate_w"], 3 * K), rows(g[pre + "time_w"], K),
        np.broadcast_to(g[pre + "gate_b"], (P, E)), np.broadcast_to(g[pre + "time_b"], (P, 2 * E))], axis=1)
    consts = np.zeros((P, C_END), np.float32)
    consts[0:B, C_TRI:C_TRI + B] = np.triu(np.ones((B, B)), 1)
    consts[:, C_IOTA:C_IOTA + NSLOT] = np.arange(NSLOT)
    consts[:, C_BIDX:C_BIDX + 32] = np.arange(P)[:, None]
    consts[:, C_ONES:C_ONES + P] = 1
    consts[:, C_EIGHTS:C_EIGHTS + SLOTS] = SLOTS * np.arange(SLOTS)
    consts[0, C_M0] = 1
    consts[1, C_M1] = 1

    nc = bacc.Bacc("TRN2", target_bir_lowering=False, num_devices=1)
    arrays, args = {}, []
    for name, a in (("x", x), ("cond", cond), ("w0", w0), ("b0", b0), ("w_exp", w_exp), ("small", small), ("consts", consts)):
        a = np.ascontiguousarray(a)
        arrays[f"in_{name}"] = a
        args.append(nc.dram_tensor(f"in_{name}", a.shape, mybir.dt.from_np(a.dtype), kind="ExternalInput").ap())
    args.append(nc.dram_tensor("out_y", (P, K, T, B), F32, kind="ExternalOutput").ap())
    cond_resid_kernel(nc, *args)
    r = run_bass_kernel_spmd(nc, [arrays], core_ids=[0])
    y = r.results[0]["out_y"]
    return np.ascontiguousarray(y.transpose(3, 2, 1, 0).reshape(B, T, K * P))
```

```python
from contextlib import ExitStack

import concourse.bass as bass
from concourse import mybir

F32 = mybir.dt.float32
F32R = mybir.dt.float32r
BF16 = mybir.dt.bfloat16
I32 = mybir.dt.int32
ALU = mybir.AluOpType
ACT = mybir.ActivationFunctionType
AX_X = mybir.AxisListType.X

P = 128
B = 64
T = 64
D = 256
K = D // P
E = 4
HID = 1024
NCH = HID // P
GT = 8
NG = T // GT
QT = 4
SLOTS = 8
HEAD = T // 3
PROP = T - 2 * HEAD
MAXG = (2 * B + (SLOTS - 1) * E) // SLOTS + 1
NSLOT = MAXG * SLOTS
PIECE = 512
WCOLS = K * HID
RING = 3

ORDER = [E, 0, 3, 1, 2]
RUNS = [(0, 1, T, T), (0, 2, 2 * HEAD, PROP), (HEAD, 1, T, T - HEAD), (0, 1, T, T)]
TOKS = [n * length for _, n, _, length in RUNS]
MASKED_EXPERT, MASKED_STEP = 1, HEAD
assert PROP == HEAD + 1

POS_AT, LIST_AT = 2, 4

C_TRI = 0
C_IOTA = C_TRI + B
C_BIDX = C_IOTA + NSLOT
C_ONES = C_BIDX + 32
C_EIGHTS = C_ONES + P
C_TWO = C_EIGHTS + SLOTS
C_LOW = C_TWO + 1
C_TIE = C_LOW + 1
C_CUM = C_TIE + E * E
C_END = C_CUM + (E + 1) * E
S_B1, S_B2, S_GW, S_TW, S_GB, S_TB = 0, 40, 50, 74, 90, 94
S_END = 102


def cond_resid_kernel(nc, x, cond, w0, b0, w_exp, small, consts, out):
    ctx = ExitStack()
    with ctx:
        def sb(name, shape, dt=F32):
            return ctx.enter_context(nc.sbuf_tensor(name, shape, dt))

        def psum(name, shape):
            return ctx.enter_context(nc.psum_tensor(name, shape, F32))

        def sem(name):
            return ctx.enter_context(nc.semaphore(name))

        acc = sb("acc", [P, K, T, B])
        x_hl = sb("x_hl", [P, 2, K, T, B], F32R)
        w_buf = [sb(f"w_buf{i}", [P, 2, 2 * WCOLS], F32R) for i in range(2)]
        shared_buf = sb("shared_buf", [P, 4096], F32R)
        xg = shared_buf[:].rearrange("p (i s k n) -> p i s k n", i=2, s=2, k=K)
        wx = shared_buf[:, 0:2048].rearrange("p (s k n) -> p s k n", s=2, k=K)
        bias0 = shared_buf[:, 2048:2560]
        ones_r = shared_buf[:, 2560:2816]
        y_all = sb("y_all", [P, 1536])
        wh = y_all[:].bitcast(BF16).rearrange("p (i k n) -> p i k n", i=3, k=K)
        y_w = y_all[:, 0:1024].rearrange("p (k n) -> p k n", k=K)
        agg = y_all[:, 640:640 + 3 * K * B].rearrange("p (i k b) -> p i k b", i=3, k=K)
        pick = y_all[0:B, 0:NSLOT]
        pick_w = y_all[0:B, NSLOT:2 * NSLOT]
        raw_w0 = acc[:, 0, 32:64, :].rearrange("p t b -> p (t b)").rearrange("p (k n) -> p k n", n=2 * D)
        raw_b0 = acc[:, 1, 32:40, :].rearrange("p t b -> p (t b)")
        stage = sb("stage", [P, RING, PIECE])
        g_f = sb("g_f", [P, 2, 512])
        g_hi = sb("g_hi", [P, 2, 512], F32R)
        g_lo = sb("g_lo", [P, 2, 512], F32R)
        uc = sb("uc", [P, 2, K, B])
        d_t = sb("d_t", [P, K, B])
        h_f = sb("h_f", [P, 2, K, B])
        h_r = sb("h_r", [P, K, B])
        h_b = sb("h_b", [P, 3, K, B], BF16)
        seg = sb("seg", [P, 3, K, B])
        par = sb("par", [P, S_END])
        con = sb("con", [P, C_END])
        turn = sb("turn", [P, 2])
        gs = sb("gs", [P, 96])
        cmp8 = h_r[:, 0, 0:E * SLOTS].rearrange("p (e s) -> p e s", e=E)
        cum = h_r[:, 1, 0:(E + 1) * E].rearrange("p (q e) -> p q e", e=E)
        slot_w = uc[:].rearrange("p i k b -> p (i k b)")[:, 0:NSLOT]
        slot_b = h_f[0:1].rearrange("p i k b -> p (i k b)")[:, 0:SLOTS + NSLOT].bitcast(I32)
        starts = sb("starts", [P, E + 1], I32)

        zy = psum("zy", [P, 3 * K, 512])
        zb = zy[:, 0:4].rearrange("p (i a) (m t b) -> p i a m t b", i=2, m=2, t=QT)
        hp = [psum(f"hp{i}", [P, 512]) for i in range(2)]
        yp = [zy[:, 4 + k] for k in range(K)]
        gp, lists = zy[:, 0], zy[:, 1]
        y_last = [zy[:, 2 + k] for k in range(K)]

        mod_f = gs[0:B, 0:8]
        logit = gs[0:B, 8:12]
        nmax = gs[0:B, 12:13]
        ex = gs[0:B, 13:17]
        esum = gs[0:B, 17:18]
        score = gs[0:B, 18:22]
        rank4 = gs[0:B, 22:38].rearrange("p (e j) -> p e j", j=E)
        tie4 = gs[0:B, 65:81].rearrange("p (e j) -> p e j", j=E)
        rank = gs[0:B, 38:42]
        sel = gs[0:B, 42:46]
        wsel = gs[0:B, 46:50]
        den = gs[0:B, 50:51]
        ngr = gs[:, 51:55]
        start_f = gs[:, 55:60]
        gslot = gs[0:B, 60:64]
        cmp_w = slot_w[0:B, :]

        s_cond, s_w0, s_b0, s_par, s_x0, s_x1, s_x2, s_out = (
            sem(n) for n in ("s_cond", "s_w0", "s_b0", "s_par", "s_x0", "s_x1", "s_x2", "s_out"))
        piece_in = [sem(f"piece_in{i}") for i in range(RING)]
        wx_hi, wx_split, wh_split, bias_ready, ones_ready = (
            sem(n) for n in ("wx_hi", "wx_split", "wh_split", "bias_ready", "ones_ready"))
        wh_half, wh_first = sem("wh_half"), sem("wh_first")
        piece_hi, piece_done = sem("piece_hi"), sem("piece_done")
        x0_hi, x0_done, xs_hi, xs_done = (sem(n) for n in ("x0_hi", "x0_done", "xs_hi", "xs_done"))
        z_done, tanh_done, d_done, q_done, h_done = (sem(n) for n in ("z_done", "tanh_done", "d_done", "q_done", "h_done"))
        h1_done, hr_done, h2_done, h3_done = (sem(n) for n in ("h1_done", "hr_done", "h2_done", "h3_done"))
        x1_sum, x1_hi, x1_done, seg_done = (sem(n) for n in ("x1_sum", "x1_hi", "x1_done", "seg_done"))
        l1_done, l2_done, y_read = sem("l1_done"), sem("l2_done"), sem("y_read")
        gelu_done, ghi_done, glo_done = sem("gelu_done"), sem("ghi_done"), sem("glo_done")
        silu_t, silu_done, mod_mm = sem("silu_t"), sem("silu_done"), sem("mod_mm")
        agg_done, gate_mm, nmax_done, exp_done = sem("agg_done"), sem("gate_mm"), sem("nmax_done"), sem("exp_done")
        sel_done, pos_mm, starts_done, pick_done, list_mm, batches_done = (
            sem(n) for n in ("sel_done", "pos_mm", "starts_done", "pick_done", "list_mm", "batches_done"))
        pick_w_done, weight_mm = sem("pick_w_done"), sem("weight_mm")
        dve_math = sem("dve_math")
        gather_done, yw_done, add_done = sem("gather_done"), sem("yw_done"), sem("add_done")
        head_ready, out_ready = sem("head_ready"), sem("out_ready")

        NP = 2 * WCOLS // PIECE

        def w_of(i):
            return w_buf[i % 2]

        def group_bounds(eng):
            eng.wait_ge(starts_done, 1)
            return [eng.value_load(starts[0:1, e:e + 1], min_val=0, max_val=MAXG) for e in range(E + 1)]

        def y_bank(r):
            return [zy[:, bass.ds(((r + 1) % 2) * K + 2 + k, 1), :].rearrange("p i n -> p (i n)") for k in range(K)]

        def pieces_at(j):
            return [[], [0], [1], [2], [3], [4], [5], [6, 7]][j]

        def tokens_of(t, e, b):
            first, n, step, length = RUNS[e]
            v = t[..., first:first + n * length, bass.ds(b, 1)]
            if len(v.shape) == 5:
                v = v.rearrange("p s k (i t) b -> p (s k) i (t b)", i=n)
            else:
                v = v.rearrange("p k (i t) b -> p k i (t b)", i=n)
            return bass.AP(v.tensor, v.offset, [list(v.ap[0]), list(v.ap[1]), [step * B, n], [B, length]])

        block = ctx.enter_context(nc.Block())

        @block.sync
        def _(sp):
            sp.dma_start(raw_w0[:, 0:K], w0[:, 0:K * 2 * D].rearrange("p (k n) -> p k n", k=K)).then_inc(s_w0, 16)
            sp.dma_start(acc[:, :, 0:GT], x[:, :, 0:GT]).then_inc(s_x0, 16)
            sp.dma_start(con[:], consts).then_inc(s_par, 16)
            sp.dma_start(par[:], small).then_inc(s_par, 16)
            sp.dma_start(acc[:, :, GT:T // 2], x[:, :, GT:T // 2]).then_inc(s_x1, 16)
            for n in range(len(ORDER) * NP):
                if n == 2:
                    sp.wait_ge(wx_split, K)
                    sp.wait_ge(wh_split, K)
                    sp.wait_ge(bias_ready, 1)
                    sp.dma_start(acc[:, :, T // 2:T], x[:, :, T // 2:T]).then_inc(s_x2, 16)
                if n >= RING:
                    sp.wait_ge(piece_done, n - RING + 1)
                e, j = ORDER[n // NP], n % NP
                sp.dma_start(stage[:, n % RING], w_exp[e, :, j * PIECE:(j + 1) * PIECE]).then_inc(piece_in[n % RING], 16)
            sp.wait_ge(head_ready, 1)
            sp.dma_start(out[:, :, 0:HEAD], acc[:, :, 0:HEAD]).then_inc(s_out, 16)
            for k in range(K):
                sp.wait_ge(out_ready, k + 1)
                sp.dma_start(out[:, k, HEAD:T], acc[:, k, HEAD:T]).then_inc(s_out, 16)
            sp.wait_ge(s_out, 16 * (1 + K))

        @block.gpsimd
        def _(pool):
            def split_x(s):
                pool.tensor_copy(x_hl[:, 0, :, bass.ds(s, 1), :], acc[:, :, bass.ds(s, 1), :]).then_inc(xs_hi, 1)
                pool.wait_ge(xs_hi, s - QT + 1)
                pool.tensor_tensor(x_hl[:, 1, :, bass.ds(s, 1), :], acc[:, :, bass.ds(s, 1), :],
                                   x_hl[:, 0, :, bass.ds(s, 1), :].bitcast(F32), ALU.subtract).then_inc(xs_done, 1)

            def add_h(s, i):
                a = acc[:, :, bass.ds(s, 1), :].rearrange("p k t b -> p k (t b)")
                hi = x_hl[:, 0, :, bass.ds(s, 1), :].rearrange("p k t b -> p k (t b)")
                lo = x_hl[:, 1, :, bass.ds(s, 1), :].rearrange("p k t b -> p k (t b)")
                sg = seg[:, bass.ds((s * 3 + 2) // 64, 1)].rearrange("p s k b -> p (s k) b")
                pool.wait_ge(h_done, s + 2)
                pool.tensor_tensor(hi, a, h_f[:, 1 - i % 2], ALU.add).then_inc(x1_hi, 1)
                pool.tensor_tensor(a, a, h_f[:, 1 - i % 2], ALU.add).then_inc(x1_sum, 1)
                pool.wait_ge(x1_sum, s + 1)
                pool.tensor_tensor(lo, a, hi.bitcast(F32), ALU.subtract).then_inc(x1_done, 1)
                pool.wait_ge(seg_done, s + 1)
                pool.tensor_tensor(sg, sg, a, ALU.add).then_inc(seg_done, 1)

            pool.memset(turn[:], 0.0).then_inc(gather_done, 1)
            pool.memset(seg[:], 0.0).then_inc(seg_done, 1)
            pool.wait_ge(s_x0, 16)
            for s in range(QT, GT):
                split_x(s)
            pool.wait_ge(s_x1, 16)
            for s in range(GT):
                split_x(s + GT)
                add_h(s, s)
            pool.wait_ge(s_x2, 16)
            with pool.Fori(1, NG - 1) as g:
                for i in range(GT):
                    split_x(g * GT + GT + i)
                    add_h(g * GT + i, i)
            for i in range(GT):
                add_h((NG - 1) * GT + i, i)
            for j in range(NCH):
                c = (NG - 1) * NCH + j
                if j == 0:
                    pool.wait_ge(glo_done, c)
                if j >= 2:
                    pool.wait_ge(l2_done, c - 1)
                pool.wait_ge(ghi_done, c + 1)
                pool.tensor_tensor(g_lo[:, j % 2], g_f[:, j % 2], g_hi[:, j % 2].bitcast(F32), ALU.subtract).then_inc(glo_done, 1)

            def gather(r, e, n):
                bs = nc.values_load_multi_w_load_instructions(slot_b[0:1, bass.ds(r * SLOTS + SLOTS, SLOTS)], engines=(mybir.EngineType.Pool,), min_val=0, max_val=B - 1)[1]
                pool.wait_ge(l1_done, (r + NG - 1) * NCH)
                pool.wait_ge(gather_done, r + 1)
                pool.tensor_tensor(turn[:, 1:2], turn[:, 0:1], turn[:, 0:1], ALU.mult)
                for s in range(SLOTS):
                    dst = xg[:, bass.ds(r % 2, 1), :, :, s * n:(s + 1) * n].rearrange(
                        "p i s k (a n) -> p (i s k) a n", a=RUNS[e][1])
                    last = pool.tensor_copy(dst, tokens_of(x_hl, e, bs[s]))
                last.then_inc(gather_done, 1)

            sv = group_bounds(pool)
            pool.wait_ge(batches_done, 1)
            for q in range(E):
                e = ORDER[q + 1]
                n = TOKS[e]
                with pool.Fori(sv[q], sv[q + 1]) as r:
                    if q == 0:
                        with pool.If(0 < r):
                            gather(r, e, n)
                    else:
                        gather(r, e, n)

        @block.scalar
        def _(act):
            def tanh(s, i, buf):
                act.wait_ge(z_done, s + 1)
                act.activation(uc[:],
                               zb[:, buf, :, :, i % QT, :], ACT.Tanh).then_inc(tanh_done, 1)

            def gelu_chunk(g, j, e, n, very_first=False):
                c = g * NCH + j
                act.wait_ge(l1_done, c + 1)
                if not very_first:
                    act.wait_ge(glo_done, c - 1)
                act.activation(g_f[:, j % 2, 0:n], hp[j % 2][:, 0:n], ACT.Gelu_apprx_tanh,
                               bias=par[:, S_B1 + e * NCH + j:S_B1 + e * NCH + j + 1]).then_inc(gelu_done, 1)
                act.wait_ge(gelu_done, c + 1)
                if not very_first:
                    act.wait_ge(l2_done, c - 1)
                act.activation(g_hi[:, j % 2, 0:n], g_f[:, j % 2, 0:n], ACT.Copy).then_inc(ghi_done, 1)

            def piece_high(n):
                c = n % NP * PIECE
                act.wait_ge(piece_in[n % RING], 16 * (n // RING + 1))
                act.activation(w_of(n // NP)[:, 0, c:c + PIECE], stage[:, n % RING], ACT.Copy).then_inc(piece_hi, 1)

            act.dma_start(h_f[:, 0], cond).then_inc(s_cond, 16)
            act.dma_start(raw_w0[:, K:2 * K], w0[:, K * 2 * D:2 * K * 2 * D].rearrange("p (k n) -> p k n", k=K)).then_inc(s_w0, 16)
            act.dma_start(raw_b0, b0).then_inc(s_b0, 16)
            act.wait_ge(ones_ready, 1)
            act.activation(gs[:, 64:65], ones_r[:, 0:1].bitcast(F32), ACT.Gelu_apprx_tanh)
            act.wait_ge(s_cond, 16)
            act.activation(uc[:, 0], h_f[:, 0], ACT.Tanh, scale=0.5).then_inc(silu_t, 1)
            act.wait_ge(s_w0, 32)
            for k in range(K):
                act.activation(wx[:, 0, k, 0:D], raw_w0[:, k, 0:D], ACT.Copy, scale=0.5)
                act.activation(wx[:, 0, k, D:2 * D], raw_w0[:, k, D:2 * D], ACT.Copy).then_inc(wx_hi, 1)
            act.wait_ge(s_x0, 16)
            act.activation(x_hl[:, 0, :, 0:QT], acc[:, :, 0:QT], ACT.Copy).then_inc(x0_hi, 1)
            act.activation(raw_w0[:, K:2 * K, 0:D], raw_w0[:, K:2 * K, 0:D], ACT.Copy, scale=0.5).then_inc(wh_half, 1)
            act.wait_ge(wh_half, 1)
            act.activation(wh[:, 0], raw_w0[:, K:2 * K], ACT.Copy).then_inc(wh_first, 1)

            for i in range(GT):
                tanh(i, i, i // QT)
                piece_high(i)
            for i in range(GT):
                tanh(GT + i, i, i // QT)
                gelu_chunk(0, i, E, 512, i < 2)
                piece_high(NP + i)
            with act.Fori(2, NG) as g:
                for i in range(GT):
                    tanh(g * GT + i, i, i // QT)
                    gelu_chunk(g - 1, i, E, 512)
            for j in range(NCH):
                if j == 1:
                    act.wait_ge(nmax_done, 1)
                    act.activation(ex, logit, ACT.Exp, bias=nmax).then_inc(exp_done, 1)
                gelu_chunk(NG - 1, j, E, 512)
            sv = group_bounds(act)
            for q in range(E):
                e = ORDER[q + 1]
                n = SLOTS * TOKS[e]
                with act.Fori(sv[q], sv[q + 1]) as r:
                    if q < E - 1:
                        with act.If(sv[q] < r):
                            for j in range(NCH):
                                gelu_chunk(r + NG, j, e, n)
                        with act.Else():
                            for j in range(NCH):
                                gelu_chunk(r + NG, j, e, n)
                                if pieces_at(j) == [0]:
                                    act.wait_ge(l2_done, (r + NG) * NCH)
                                for m in pieces_at(j):
                                    piece_high((q + 2) * NP + m)
                    else:
                        for j in range(NCH):
                            gelu_chunk(r + NG, j, e, n)

        @block.vector
        def _(dve):
            count = [0]

            def link(ins):
                count[0] += 1
                ins.then_inc(dve_math, 1)
                dve.wait_ge(dve_math, count[0])

            def split_lo(g, j, n):
                c = g * NCH + j
                dve.wait_ge(ghi_done, c + 1)
                dve.tensor_tensor(g_lo[:, j % 2, 0:n], g_f[:, j % 2, 0:n], g_hi[:, j % 2, 0:n].bitcast(F32),
                                  ALU.subtract).then_inc(glo_done, 1)

            def piece_low(n):
                w = w_of(n // NP)
                c = n % NP * PIECE
                dve.wait_ge(piece_hi, n + 1)
                dve.tensor_tensor(w[:, 1, c:c + PIECE], stage[:, n % RING], w[:, 0, c:c + PIECE].bitcast(F32),
                                  ALU.subtract).then_inc(piece_done, 1)

            def split_state(s, h):
                dve.wait_ge(h1_done, s + 2)
                dve.wait_ge(h_done, s + 2)
                dve.tensor_tensor(h_r[:], h, h_b[:, 0], ALU.subtract).then_inc(hr_done, 1)
                dve.wait_ge(hr_done, s + 2)
                dve.tensor_copy(h_b[:, 1], h_r[:]).then_inc(h2_done, 1)
                dve.wait_ge(h2_done, s + 2)
                dve.tensor_tensor(h_b[:, 2], h_r[:], h_b[:, 1], ALU.subtract).then_inc(h3_done, 1)

            def cell(s, i, first=False):
                dve.wait_ge(tanh_done, s + 1)
                dve.wait_ge(h_done, s + 1)
                dve.tensor_tensor(d_t[:], h_f[:, i % 2], uc[:, 1], ALU.subtract).then_inc(d_done, 1)
                dve.wait_ge(d_done, s + 1)
                dve.scalar_tensor_tensor(out=d_t[:], in0=uc[:, 0], scalar=1.0, in1=d_t[:],
                                         op0=ALU.add, op1=ALU.mult).then_inc(q_done, 1)
                dve.wait_ge(q_done, s + 1)
                dve.scalar_tensor_tensor(out=h_b[:, 0], in0=d_t[:], scalar=0.5, in1=uc[:, 1],
                                         op0=ALU.mult, op1=ALU.add).then_inc(h1_done, 1)
                if not first:
                    dve.wait_ge(x1_sum, s)
                dve.scalar_tensor_tensor(out=h_f[:, 1 - i % 2], in0=d_t[:], scalar=0.5, in1=uc[:, 1],
                                         op0=ALU.mult, op1=ALU.add).then_inc(h_done, 1)
                split_state(s, h_f[:, 1 - i % 2])

            def shared_out(g, y):
                dve.wait_ge(l2_done, (g + 1) * NCH)
                dve.wait_ge(x1_done, (g + 1) * GT)
                for k in range(K):
                    a = acc[:, k, bass.ds(g * GT, GT), :].rearrange("p t b -> p (t b)")
                    last = dve.scalar_tensor_tensor(out=a, in0=y[k], scalar=par[:, S_B2 + E * K + k:S_B2 + E * K + k + 1],
                                                    in1=a, op0=ALU.add, op1=ALU.add)
                last.then_inc(y_read, 1)

            dve.memset(ones_r.bitcast(F32), 1.0).then_inc(ones_ready, 1)
            dve.wait_ge(s_cond, 16)
            dve.tensor_copy(h_b[:, 0], h_f[:, 0]).then_inc(h1_done, 1)
            dve.sem_inc(h_done, 1)
            split_state(-1, h_f[:, 0])
            dve.wait_ge(silu_t, 1)
            link(dve.scalar_tensor_tensor(out=uc[:, 1], in0=uc[:, 0], scalar=1.0, in1=h_f[:, 0], op0=ALU.add, op1=ALU.mult))
            dve.tensor_scalar(d_t[:], uc[:, 1], 0.5, None, ALU.mult).then_inc(silu_done, 1)
            for k in range(K):
                dve.wait_ge(wx_hi, k + 1)
                for a, scale in ((0, 0.5), (D, 1.0)):
                    last = dve.scalar_tensor_tensor(out=wx[:, 1, k, a:a + D], in0=raw_w0[:, k, a:a + D], scalar=scale,
                                                    in1=wx[:, 0, k, a:a + D].bitcast(F32), op0=ALU.mult, op1=ALU.subtract)
                last.then_inc(wx_split, 1)
            dve.wait_ge(s_b0, 16)
            dve.wait_ge(s_par, 32)
            two, low = con[:, C_TWO:C_TWO + 1], con[:, C_LOW:C_LOW + 1]
            link(dve.tensor_scalar(raw_b0[:, 0:D], raw_b0[:, 0:D], two, 0.5, ALU.add, ALU.mult))
            link(dve.tensor_copy(bias0, raw_b0))
            dve.scalar_tensor_tensor(out=bias0, in0=bias0.bitcast(F32), scalar=low, in1=raw_b0,
                                     op0=ALU.mult, op1=ALU.add).then_inc(bias_ready, 1)
            dve.wait_ge(x0_hi, 1)
            dve.tensor_tensor(x_hl[:, 1, :, 0:QT].rearrange("p k t b -> p k (t b)"),
                              acc[:, :, 0:QT].rearrange("p k t b -> p k (t b)"),
                              x_hl[:, 0, :, 0:QT].rearrange("p k t b -> p k (t b)").bitcast(F32), ALU.subtract).then_inc(x0_done, 1)
            dve.wait_ge(wh_first, 1)
            for k in range(K):
                raw = raw_w0[:, K + k]
                link(dve.tensor_tensor(raw, raw, wh[:, 0, k], ALU.subtract))
                link(dve.tensor_copy(wh[:, 1, k], raw))
                dve.tensor_tensor(wh[:, 2, k], raw, wh[:, 1, k], ALU.subtract).then_inc(wh_split, 1)
            dve.wait_ge(mod_mm, 1)
            dve.tensor_tensor(mod_f, hp[0][0:B, 0:8], par[0:B, S_TB:S_TB + 8], ALU.add)

            for i in range(GT):
                cell(i, i, i == 0)
                piece_low(i)
            for i in range(GT):
                cell(GT + i, i)
                split_lo(0, i, 512)
                piece_low(NP + i)
            with dve.Fori(2, NG) as g:
                for i in range(GT):
                    if i == 2:
                        shared_out(g - 2, yp)
                    cell(g * GT + i, i)
                    split_lo(g - 1, i, 512)

            def gate_means():
                dve.wait_ge(seg_done, T + 1)
                link(dve.tensor_tensor(agg[:, 1], seg[:, 0], seg[:, 2], ALU.add))
                link(dve.tensor_tensor(agg[:, 0], agg[:, 1], seg[:, 1], ALU.add))
                link(dve.tensor_tensor(agg[:, 2], seg[:, 1], seg[:, 2], ALU.add))
                link(dve.tensor_scalar(agg[:, 0], agg[:, 0], 1.0 / T, None, ALU.mult))
                dve.tensor_scalar(agg[:, 1:3], agg[:, 1:3], 1.0 / (HEAD + PROP), None, ALU.mult).then_inc(agg_done, 1)

            def gate_logits():
                dve.wait_ge(gate_mm, 1)
                link(dve.tensor_tensor(logit, gp[0:B, 0:E], par[0:B, S_GB:S_GB + E], ALU.add))
                link(dve.scalar_tensor_tensor(out=logit, in0=mod_f[:, 0:E], scalar=1.0, in1=logit, op0=ALU.add, op1=ALU.mult))
                link(dve.tensor_tensor(logit, logit, mod_f[:, E:2 * E], ALU.add))
                link(dve.tensor_reduce(nmax, logit, AX_X, ALU.max))
                dve.tensor_scalar(nmax, nmax, -1.0, None, ALU.mult).then_inc(nmax_done, 1)

            def gate_choice():
                dve.wait_ge(exp_done, 1)
                link(dve.tensor_reduce(esum, ex, AX_X, ALU.add))
                link(dve.reciprocal(esum, esum))
                link(dve.tensor_scalar(score, ex, esum, None, ALU.mult))
                of_j = score.unsqueeze(1).to_broadcast([B, E, E])
                of_e = score.unsqueeze(2).to_broadcast([B, E, E])
                tie = con[0:B, C_TIE:C_TIE + E * E].rearrange("p (e j) -> p e j", j=E)
                dve.tensor_tensor(rank4, of_j, of_e, ALU.is_gt)
                link(dve.tensor_tensor(tie4, of_j, of_e, ALU.is_equal))
                link(dve.tensor_tensor(tie4, tie4, tie, ALU.mult))
                link(dve.tensor_tensor(rank4, rank4, tie4, ALU.add))
                link(dve.tensor_reduce(rank, rank4, AX_X, ALU.add))
                dve.tensor_scalar(sel, rank, 1.5, None, ALU.is_lt).then_inc(sel_done, 1)
                dve.wait_ge(sel_done, 1)
                link(dve.tensor_tensor(wsel, sel, score, ALU.mult))
                link(dve.tensor_reduce(den, wsel, AX_X, ALU.add))
                link(dve.tensor_scalar(den, den, 1e-8, None, ALU.add))
                link(dve.reciprocal(den, den))
                link(dve.tensor_scalar(wsel, wsel, den, None, ALU.mult))

            def gate_slots():
                dve.wait_ge(pos_mm, 1)
                link(dve.tensor_copy(ngr, gp[:, 2 * E:3 * E]))
                link(dve.tensor_tensor(cmp8[:], ngr.unsqueeze(2).to_broadcast([P, E, SLOTS]),
                                       con[:, C_EIGHTS:C_EIGHTS + SLOTS].unsqueeze(1).to_broadcast([P, E, SLOTS]), ALU.is_gt))
                link(dve.tensor_reduce(ngr, cmp8[:], AX_X, ALU.add))
                link(dve.tensor_scalar(ngr, ngr, 1.0, None, ALU.max))
                link(dve.tensor_tensor(cum[:], ngr.unsqueeze(1).to_broadcast([P, E + 1, E]),
                                       con[:, C_CUM:C_CUM + (E + 1) * E].rearrange("p (q j) -> p q j", j=E), ALU.mult))
                link(dve.tensor_reduce(start_f, cum[:], AX_X, ALU.add))
                dve.tensor_copy(starts[:], start_f).then_inc(starts_done, 1)
                link(dve.tensor_scalar(gslot, start_f[0:B, 0:E], float(SLOTS), 4096.0, ALU.mult, ALU.add))
                link(dve.scalar_tensor_tensor(out=gslot, in0=sel, scalar=-4096.0, in1=gslot, op0=ALU.mult, op1=ALU.add))
                link(dve.tensor_tensor(gslot, gslot, gp[0:B, E:2 * E], ALU.add))
                link(dve.tensor_scalar(pick, iota, gslot[:, 0:1], None, ALU.is_equal))
                for q in range(1, E):
                    last = dve.scalar_tensor_tensor(out=pick, in0=iota, scalar=gslot[:, q:q + 1], in1=pick,
                                                    op0=ALU.is_equal, op1=ALU.add)
                    if q < E - 1:
                        link(last)
                last.then_inc(pick_done, 1)

            def gate_weights():
                link(dve.tensor_scalar(pick_w, iota, gslot[:, 0:1], wsel[:, 0:1], ALU.is_equal, ALU.mult))
                for q in range(1, E):
                    link(dve.tensor_scalar(cmp_w, iota, gslot[:, q:q + 1], wsel[:, q:q + 1], ALU.is_equal, ALU.mult))
                    last = dve.tensor_tensor(pick_w, pick_w, cmp_w, ALU.add)
                    if q < E - 1:
                        link(last)
                last.then_inc(pick_w_done, 1)

            def gather_first():
                n = TOKS[ORDER[1]]
                bs = nc.values_load_multi_w_load_instructions(slot_b[0:1, SLOTS:2 * SLOTS], engines=(mybir.EngineType.DVE,), min_val=0, max_val=B - 1)[1]
                for s in range(SLOTS):
                    dst = xg[:, 0, :, :, s * n:(s + 1) * n].rearrange("p s k (a n) -> p (s k) a n", a=RUNS[ORDER[1]][1])
                    last = dve.tensor_copy(dst, tokens_of(x_hl, ORDER[1], bs[s]))
                last.then_inc(gather_done, 1)

            iota = con[0:B, C_IOTA:C_IOTA + NSLOT]
            gate_means()
            gate_logits()
            gate_choice()
            gate_slots()
            shared_out(NG - 2, yp)
            dve.wait_ge(list_mm, 1)
            dve.tensor_copy(slot_b[0:1, SLOTS:SLOTS + NSLOT], lists[0:1, 0:NSLOT]).then_inc(batches_done, 1)
            dve.wait_ge(batches_done, 1)
            gather_first()
            gate_weights()
            sv = group_bounds(dve)

            def weigh(r, e):
                n = TOKS[e]
                dve.wait_ge(l2_done, (r + NG + 1) * NCH)
                dve.wait_ge(add_done, (r + 1) * SLOTS + 1)
                ws = slot_w[:, bass.ds(r * SLOTS, SLOTS)].unsqueeze(2).to_broadcast([P, SLOTS, n])
                for k in range(K):
                    dve.scalar_tensor_tensor(
                        out=y_w[:, k, 0:SLOTS * n].rearrange("p (s n) -> p s n", n=n),
                        in0=y_bank(r)[k][:, 0:SLOTS * n].rearrange("p (s n) -> p s n", n=n),
                        scalar=par[:, S_B2 + e * K + k:S_B2 + e * K + k + 1], in1=ws,
                        op0=ALU.add, op1=ALU.mult).then_inc(yw_done, 1)
                dve.wait_ge(yw_done, (r + 1) * K)
                if e == MASKED_EXPERT:
                    dve.memset(y_w[:, :, 0:SLOTS * n].rearrange("p k (s n) -> p k s n", n=n)[:, :, :, MASKED_STEP],
                               0.0).then_inc(y_read, 1)
                else:
                    dve.sem_inc(y_read, 1)

            def add_slots(r, e, slots):
                n = TOKS[e]
                bs = nc.values_load_multi_w_load_instructions(slot_b[0:1, bass.ds(r * SLOTS + slots[0], len(slots))], engines=(mybir.EngineType.DVE,), min_val=0, max_val=B - 1)[1]
                for s, b in zip(slots, bs):
                    if s == 0:
                        dve.wait_ge(y_read, r + NG)
                    dve.wait_ge(add_done, r * SLOTS + s + 1)
                    dst = tokens_of(acc, e, b)
                    dve.tensor_tensor(dst, dst, y_w[:, :, s * n:(s + 1) * n].rearrange("p k (a n) -> p k a n", a=RUNS[e][1]),
                                      ALU.add).then_inc(add_done, 1)

            def batches(r, a, n):
                return nc.values_load_multi_w_load_instructions(
                    slot_b[0:1, bass.ds((r + 1) * SLOTS + a, n)], engines=(mybir.EngineType.DVE,), min_val=0, max_val=B - 1)[1]

            def add_last(r, e, bs):
                n = TOKS[e]
                dve.wait_ge(y_read, r + NG + 1)
                for k in range(K):
                    for s in range(SLOTS):
                        dve.wait_ge(add_done, (r + 1 + k) * SLOTS + s + 1)
                        dst = tokens_of(acc[:, k:k + 1], e, bs[s])
                        src = y_w[:, k:k + 1, s * n:(s + 1) * n].rearrange("p k (a n) -> p k a n", a=RUNS[e][1])
                        dve.tensor_tensor(dst, dst, src, ALU.add).then_inc(add_done, 1)
                    dve.wait_ge(add_done, (r + 2 + k) * SLOTS + 1)
                    dve.sem_inc(out_ready, 1)

            n0 = SLOTS * TOKS[ORDER[1]]
            dve.wait_ge(glo_done, NG * NCH)
            split_lo(NG, 0, n0)
            shared_out(NG - 1, y_last)
            dve.wait_ge(y_read, NG)
            dve.sem_inc(add_done, SLOTS + 1)
            split_lo(NG, 1, n0)
            dve.wait_ge(weight_mm, 1)
            dve.tensor_copy(slot_w[:], lists[:, NSLOT:2 * NSLOT])
            for q in range(E):
                e = ORDER[q + 1]
                n = SLOTS * TOKS[e]
                with dve.Fori(sv[q], sv[q + 1]) as r:
                    common = NCH - 2 if q == E - 1 else NCH
                    with dve.If(sv[q] < r):
                        for j in range(2, common):
                            split_lo(r + NG, j, n)
                            if j < 2 + SLOTS // 2:
                                add_slots(r, e, [2 * j - 4, 2 * j - 3])
                    with dve.Else():
                        for j in range(2, common):
                            split_lo(r + NG, j, n)
                            if q == E - 1:
                                add_slots(r, ORDER[q], [2 * j - 4, 2 * j - 3])
                            elif q and 3 <= j < 3 + SLOTS // 2:
                                add_slots(r, ORDER[q], [2 * j - 6, 2 * j - 5])
                            if q < E - 1:
                                for m in (pieces_at(1) if j == 2 else []) + pieces_at(j):
                                    piece_low((q + 2) * NP + m)
                        if q == E - 1:
                            dve.wait_ge(add_done, (r + 1) * SLOTS + 1)
                            dve.sem_inc(head_ready, 1)
                    bs = []
                    for j in range(common, NCH):
                        split_lo(r + NG, j, n)
                        bs += batches(r, len(bs), SLOTS - 2 if bs else 2)
                    with dve.If(r + 1 < sv[q + 1]):
                        split_lo(r + NG + 1, 0, n)
                        weigh(r, e)
                        split_lo(r + NG + 1, 1, n)
                    with dve.Else():
                        nn = SLOTS * TOKS[ORDER[q + 2]] if q < E - 1 else 0
                        if nn:
                            split_lo(r + NG + 1, 0, nn)
                        weigh(r, e)
                        if nn:
                            split_lo(r + NG + 1, 1, nn)
                        else:
                            add_last(r, e, bs)
        @block.tensor
        def _(pe):
            def mm(out_, lhsT, rhs, start, stop=False):
                return pe.matmul(out_, lhsT=lhsT, rhs=rhs, start=start, stop=stop, skip_group_check=True)

            def x_part(s, buf, m):
                c = slice(m * P, (m + 1) * P)
                o = zb[:, buf, m // 2, m % 2].rearrange("p t b -> p (t b)")
                mm(o, bias0[:, c], ones_r, m % 2 == 0)
                for k in range(K):
                    hi = x_hl[:, 0, k, bass.ds(s, QT), :]
                    lo = x_hl[:, 1, k, bass.ds(s, QT), :]
                    mm(o, wx[:, 0, k, c], hi, False)
                    mm(o, wx[:, 1, k, c], hi, False)
                    mm(o, wx[:, 0, k, c], lo, False)

            def h_part(s, i, buf):
                for a, ready in enumerate((h1_done, h2_done, h3_done)):
                    pe.wait_ge(ready, s + 1)
                    for m in range(2 * K):
                        o = zb[:, buf, m // 2, m % 2, i % QT, :]
                        for k in range(K):
                            for b in range(3 - a):
                                last = mm(o, wh[:, b, k, m * P:(m + 1) * P], h_b[:, a, k], False, a == 2)
                last.then_inc(z_done, 1)

            def layer1(g, j, w, src, n, very_first=False):
                c = g * NCH + j
                if not very_first:
                    pe.wait_ge(gelu_done, c - 1)
                for k in range(K):
                    o = k * HID + j * P
                    hi, lo = src(0, k), src(1, k)
                    mm(hp[j % 2][:, 0:n], w[:, 0, o:o + P], hi, k == 0)
                    mm(hp[j % 2][:, 0:n], w[:, 1, o:o + P], hi, False)
                    last = mm(hp[j % 2][:, 0:n], w[:, 0, o:o + P], lo, False, k == K - 1)
                last.then_inc(l1_done, 1)

            def layer2(g, j, w, y, n):
                c = g * NCH + j
                pe.wait_ge(ghi_done, c + 1)
                for m in range(K):
                    o = WCOLS + j * D + m * P
                    mm(y[m][:, 0:n], w[:, 0, o:o + P], g_hi[:, j % 2, 0:n], j == 0)
                    mm(y[m][:, 0:n], w[:, 1, o:o + P], g_hi[:, j % 2, 0:n], False)
                pe.wait_ge(glo_done, c + 1)
                for m in range(K):
                    o = WCOLS + j * D + m * P
                    last = mm(y[m][:, 0:n], w[:, 0, o:o + P], g_lo[:, j % 2, 0:n], False, j == NCH - 1)
                last.then_inc(l2_done, 1)

            def group_src(g):
                return lambda part, k: x_hl[:, part, k, bass.ds(g * GT, GT), :]

            y0 = yp

            pe.wait_ge(wx_split, K)
            pe.wait_ge(bias_ready, 1)
            pe.wait_ge(x0_done, 1)
            for m in range(2 * K):
                x_part(0, 0, m)
            pe.wait_ge(silu_done, 1)
            pe.wait_ge(s_par, 32)
            for k in range(K):
                last = mm(hp[0][0:B, 0:2 * E], d_t[:, k], par[:, S_TW + 2 * E * k:S_TW + 2 * E * (k + 1)], k == 0, k == K - 1)
            last.then_inc(mod_mm, 1)
            pe.wait_ge(wh_split, K)

            def steps(g, filler, carry, last_group=False):
                for i in range(GT):
                    s = g * GT + i
                    h_part(s, i, i // QT)
                    if not (last_group and i >= QT):
                        if i % QT == 0:
                            if not (isinstance(g, int) and g == 0 and i == 0):
                                pe.wait_ge(tanh_done, s)
                            pe.wait_ge(xs_done, s + QT)
                        x_part(s - i % QT + QT, (i // QT + 1) % 2, i % QT)
                    if filler:
                        f = g - 1
                        if i == 0:
                            pe.wait_ge(x1_done, g * GT)
                        layer1(f, i, w_of(0), group_src(f), 512, not carry and i < 2)
                        if i == 2 and not carry:
                            pe.wait_ge(piece_done, NP)
                        if i == 2 and carry:
                            pe.wait_ge(y_read, f)
                        if i >= 2:
                            layer2(f, i - 2, w_of(0), y0, 512)
                        elif carry:
                            layer2(f - 1, NCH - 2 + i, w_of(0), y0, 512)

            steps(0, False, False)
            pe.wait_ge(piece_done, NP // 2)
            steps(1, True, False)
            with pe.Fori(2, NG - 1) as g:
                steps(g, True, True)
            steps(NG - 1, True, True, True)
            f = NG - 1
            pe.wait_ge(x1_done, T)
            for j in range(NCH):
                layer1(f, j, w_of(0), group_src(f), 512)
                if j >= 2:
                    layer2(f, j - 2, w_of(0), y_last, 512)
                else:
                    layer2(f - 1, NCH - 2 + j, w_of(0), y0, 512)
                if j == 0:
                    pe.wait_ge(agg_done, 1)
                    for i in range(3):
                        for k in range(K):
                            a = i * K + k
                            last = mm(gp[0:B, 0:E], agg[:, i, k], par[:, S_GW + E * a:S_GW + E * (a + 1)],
                                      a == 0, a == 3 * K - 1)
                    last.then_inc(gate_mm, 1)
                if j == POS_AT:
                    pe.wait_ge(sel_done, 1)
                    mm(gp[:, 2 * E:3 * E], con[0:B, C_ONES:C_ONES + P], sel, True, True)
                    mm(gp[0:B, E:2 * E], con[0:B, C_TRI:C_TRI + B], sel, False, True).then_inc(pos_mm, 1)
                if j == LIST_AT:
                    pe.wait_ge(pick_done, 1)
                    mm(lists[0:32, 0:NSLOT], con[0:B, C_BIDX:C_BIDX + 32], pick, True, True).then_inc(list_mm, 1)

            sv = group_bounds(pe)

            def src_of(r, n):
                return lambda part, k: xg[:, bass.ds(r % 2, 1), part, k, 0:n].rearrange("p i n -> p (i n)")

            def turnover(r, i, n, w, y, r2, n2, w2):
                if n2:
                    pe.wait_ge(piece_done, i * NP + NP // 2)
                    pe.wait_ge(gather_done, r2 + 2)
                for j in range(2):
                    if n2:
                        layer1(r2 + NG, j, w2, src_of(r2, n2), n2)
                    layer2(r + NG, NCH - 2 + j, w, y, n)

            n0 = SLOTS * TOKS[ORDER[1]]
            turnover(-1, 1, 512, w_of(0), y_last, 0, n0, w_of(1))
            pe.wait_ge(pick_w_done, 1)
            mm(lists[:, NSLOT:2 * NSLOT], con[0:B, C_ONES:C_ONES + P], pick_w, True, True).then_inc(weight_mm, 1)
            for q in range(E):
                n = SLOTS * TOKS[ORDER[q + 1]]
                w = w_of(q + 1)
                with pe.Fori(sv[q], sv[q + 1]) as r:
                    y = y_bank(r)
                    for j in range(2, NCH):
                        layer1(r + NG, j, w, src_of(r, n), n)
                        if j == 2:
                            pe.wait_ge(y_read, r + NG - 1)
                            pe.wait_ge(piece_done, (q + 2) * NP)
                        layer2(r + NG, j - 2, w, y, n)
                    with pe.If(r + 1 < sv[q + 1]):
                        turnover(r, q + 1, n, w, y, r + 1, n, w)
                    with pe.Else():
                        if q < E - 1:
                            turnover(r, q + 2, n, w, y, r + 1, SLOTS * TOKS[ORDER[q + 2]], w_of(q + 2))
                        else:
                            turnover(r, 0, n, w, y, r + 1, 0, None)



def kernel(**inputs):
    import numpy as np
    import concourse.bacc as bacc
    from concourse.bass_utils import run_bass_kernel_spmd

    def rows(a, n):
        a = np.asarray(a)
        return np.ascontiguousarray(a.reshape(n, P, -1).transpose(1, 0, 2).reshape(P, -1))

    g = {k: np.asarray(v) for k, v in inputs.items()}
    pre = "L1_cond_"
    x = g["x"].transpose(2, 1, 0).reshape(K, P, T, B).transpose(1, 0, 2, 3)
    cond = g["cond_1024"].T.reshape(K, P, B).transpose(1, 0, 2)
    w0 = rows(g["L0_cond_weight"], 2 * K)
    b0 = np.zeros((P, 2 * D), np.float32)
    b0[0:2] = g["L0_cond_bias"]
    w1 = list(g[pre + "ew1"]) + [g[pre + "sw1"]]
    w2 = list(g[pre + "ew2"]) + [g[pre + "sw2"]]
    w_exp = np.stack([np.concatenate([rows(a, K), rows(b, NCH)], axis=1) for a, b in zip(w1, w2)])
    b1 = np.concatenate([rows(a, NCH) for a in [*g[pre + "eb1"], g[pre + "sb1"]]], axis=1)
    b2 = np.concatenate([rows(a, K) for a in [*g[pre + "eb2"], g[pre + "sb2"]]], axis=1)
    routed = np.array(ORDER[1:])
    both = np.concatenate([routed, E + routed])
    small = np.concatenate([
        b1, b2, rows(g[pre + "gate_w"][:, routed], 3 * K), rows(g[pre + "time_w"][:, both], K),
        np.broadcast_to(g[pre + "gate_b"][routed], (P, E)), np.broadcast_to(g[pre + "time_b"][both], (P, 2 * E))], axis=1)
    consts = np.zeros((P, C_END), np.float32)
    consts[0:B, C_TRI:C_TRI + B] = np.triu(np.ones((B, B)), 1)
    consts[:, C_IOTA:C_IOTA + NSLOT] = np.arange(NSLOT)
    consts[:, C_BIDX:C_BIDX + 32] = np.arange(P)[:, None]
    consts[:, C_ONES:C_ONES + P] = 1
    consts[:, C_EIGHTS:C_EIGHTS + SLOTS] = SLOTS * np.arange(SLOTS)
    consts[0:2, C_TWO] = 1
    consts[1, C_LOW] = -1
    consts[:, C_TIE:C_TIE + E * E] = (routed[None, :] < routed[:, None]).ravel()
    consts[:, C_CUM:C_CUM + (E + 1) * E] = np.tril(np.ones((E + 1, E)), -1).ravel()

    nc = bacc.Bacc("TRN2", target_bir_lowering=False, num_devices=1)
    arrays, args = {}, []
    for name, a in (("x", x), ("cond", cond), ("w0", w0), ("b0", b0), ("w_exp", w_exp), ("small", small), ("consts", consts)):
        a = np.ascontiguousarray(a)
        arrays[f"in_{name}"] = a
        args.append(nc.dram_tensor(f"in_{name}", a.shape, mybir.dt.from_np(a.dtype), kind="ExternalInput").ap())
    args.append(nc.dram_tensor("out_y", (P, K, T, B), F32, kind="ExternalOutput").ap())
    cond_resid_kernel(nc, *args)
    r = run_bass_kernel_spmd(nc, [arrays], core_ids=[0])
    y = r.results[0]["out_y"]
    return np.ascontiguousarray(y.transpose(3, 2, 1, 0).reshape(B, T, K * P))
```
